# Optimizing a Trainium2 kernel written in Bass

```python
import numpy as np
import jax
import jax.numpy as jnp

def _softmax(x, axis=-1):
    return jax.nn.softmax(x, axis=axis)

def _gelu(x):
    return jax.nn.gelu(x, approximate=True)

def _silu(x):
    return jax.nn.silu(x)

def _sigmoid(x):
    return jax.nn.sigmoid(x)

def _layernorm(x, axis=-1, eps=1e-05):
    m = jnp.mean(x, axis=axis, keepdims=True)
    v = jnp.var(x, axis=axis, keepdims=True)
    return (x - m) / jnp.sqrt(v + eps)

def _scatter_add(tgt, idx, src, axis=0):
    return tgt.at[idx].add(src)

def _segment_sum(src, seg, n):
    return jax.ops.segment_sum(src, seg, n)
kernel_name = 'mk_dlrm_tower_d1_rec_r8_c6c21e'

def setup_inputs(seed: int=0):
    np.random.seed(seed)
    _w = jnp.asarray

    def _rec_inputs():
        import jax
        import jax.numpy as jnp
        _tk = jax.random.key(seed)
        dense_ctx = jax.random.normal(jax.random.fold_in(_tk, 190), (2048, 16), jnp.float32)
        ids = jnp.stack([jax.random.randint(jax.random.fold_in(_tk, 200 + f), (2048,), 0, v, jnp.int32) for f, v in enumerate([125000, 1250, 125000, 12500, 12500, 1000, 12500, 12500, 125000, 12500, 125000, 1000, 12500, 1000, 1250, 1250, 1000, 1250, 1000, 1000, 125000, 1250, 12500, 125000, 1000, 12500, 1000, 1250, 1250, 1000, 1250, 1250, 125000, 125000, 1250, 1250, 125000, 12500, 1250])], axis=1)
        tbl_0 = 0.05 * jax.random.normal(jax.random.fold_in(_tk, 500 + 0), (125000, 16), jnp.float32)
        tbl_1 = 0.05 * jax.random.normal(jax.random.fold_in(_tk, 500 + 1), (1250, 16), jnp.float32)
        tbl_2 = 0.05 * jax.random.normal(jax.random.fold_in(_tk, 500 + 2), (125000, 16), jnp.float32)
        tbl_3 = 0.05 * jax.random.normal(jax.random.fold_in(_tk, 500 + 3), (12500, 16), jnp.float32)
        tbl_4 = 0.05 * jax.random.normal(jax.random.fold_in(_tk, 500 + 4), (12500, 16), jnp.float32)
        tbl_5 = 0.05 * jax.random.normal(jax.random.fold_in(_tk, 500 + 5), (1000, 16), jnp.float32)
        tbl_6 = 0.05 * jax.random.normal(jax.random.fold_in(_tk, 500 + 6), (12500, 16), jnp.float32)
        tbl_7 = 0.05 * jax.random.normal(jax.random.fold_in(_tk, 500 + 7), (12500, 16), jnp.float32)
        tbl_8 = 0.05 * jax.random.normal(jax.random.fold_in(_tk, 500 + 8), (125000, 16), jnp.float32)
        tbl_9 = 0.05 * jax.random.normal(jax.random.fold_in(_tk, 500 + 9), (12500, 16), jnp.float32)
        tbl_10 = 0.05 * jax.random.normal(jax.random.fold_in(_tk, 500 + 10), (125000, 16), jnp.float32)
        tbl_11 = 0.05 * jax.random.normal(jax.random.fold_in(_tk, 500 + 11), (1000, 16), jnp.float32)
        tbl_12 = 0.05 * jax.random.normal(jax.random.fold_in(_tk, 500 + 12), (12500, 16), jnp.float32)
        tbl_13 = 0.05 * jax.random.normal(jax.random.fold_in(_tk, 500 + 13), (1000, 16), jnp.float32)
        tbl_14 = 0.05 * jax.random.normal(jax.random.fold_in(_tk, 500 + 14), (1250, 16), jnp.float32)
        tbl_15 = 0.05 * jax.random.normal(jax.random.fold_in(_tk, 500 + 15), (1250, 16), jnp.float32)
        tbl_16 = 0.05 * jax.random.normal(jax.random.fold_in(_tk, 500 + 16), (1000, 16), jnp.float32)
        tbl_17 = 0.05 * jax.random.normal(jax.random.fold_in(_tk, 500 + 17), (1250, 16), jnp.float32)
        tbl_18 = 0.05 * jax.random.normal(jax.random.fold_in(_tk, 500 + 18), (1000, 16), jnp.float32)
        tbl_19 = 0.05 * jax.random.normal(jax.random.fold_in(_tk, 500 + 19), (1000, 16), jnp.float32)
        tbl_20 = 0.05 * jax.random.normal(jax.random.fold_in(_tk, 500 + 20), (125000, 16), jnp.float32)
        tbl_21 = 0.05 * jax.random.normal(jax.random.fold_in(_tk, 500 + 21), (1250, 16), jnp.float32)
        tbl_22 = 0.05 * jax.random.normal(jax.random.fold_in(_tk, 500 + 22), (12500, 16), jnp.float32)
        tbl_23 = 0.05 * jax.random.normal(jax.random.fold_in(_tk, 500 + 23), (125000, 16), jnp.float32)
        tbl_24 = 0.05 * jax.random.normal(jax.random.fold_in(_tk, 500 + 24), (1000, 16), jnp.float32)
        tbl_25 = 0.05 * jax.random.normal(jax.random.fold_in(_tk, 500 + 25), (12500, 16), jnp.float32)
        tbl_26 = 0.05 * jax.random.normal(jax.random.fold_in(_tk, 500 + 26), (1000, 16), jnp.float32)
        tbl_27 = 0.05 * jax.random.normal(jax.random.fold_in(_tk, 500 + 27), (1250, 16), jnp.float32)
        tbl_28 = 0.05 * jax.random.normal(jax.random.fold_in(_tk, 500 + 28), (1250, 16), jnp.float32)
        tbl_29 = 0.05 * jax.random.normal(jax.random.fold_in(_tk, 500 + 29), (1000, 16), jnp.float32)
        tbl_30 = 0.05 * jax.random.normal(jax.random.fold_in(_tk, 500 + 30), (1250, 16), jnp.float32)
        tbl_31 = 0.05 * jax.random.normal(jax.random.fold_in(_tk, 500 + 31), (1250, 16), jnp.float32)
        tbl_32 = 0.05 * jax.random.normal(jax.random.fold_in(_tk, 500 + 32), (125000, 16), jnp.float32)
        tbl_33 = 0.05 * jax.random.normal(jax.random.fold_in(_tk, 500 + 33), (125000, 16), jnp.float32)
        tbl_34 = 0.05 * jax.random.normal(jax.random.fold_in(_tk, 500 + 34), (1250, 16), jnp.float32)
        tbl_35 = 0.05 * jax.random.normal(jax.random.fold_in(_tk, 500 + 35), (1250, 16), jnp.float32)
        tbl_36 = 0.05 * jax.random.normal(jax.random.fold_in(_tk, 500 + 36), (125000, 16), jnp.float32)
        tbl_37 = 0.05 * jax.random.normal(jax.random.fold_in(_tk, 500 + 37), (12500, 16), jnp.float32)
        tbl_38 = 0.05 * jax.random.normal(jax.random.fold_in(_tk, 500 + 38), (1250, 16), jnp.float32)
        _rk = jax.random.fold_in(_tk, 7)
        W_top1 = 0.0606339 * jax.random.normal(jax.random.fold_in(_tk, 801), (272, 512), jnp.float32)
        W_top2 = 0.0441942 * jax.random.normal(jax.random.fold_in(_tk, 802), (512, 256), jnp.float32)
        W_top3 = 0.0625 * jax.random.normal(jax.random.fold_in(_tk, 803), (256, 1), jnp.float32)
        b_top1 = jnp.zeros((512,), jnp.float32)
        b_top2 = jnp.zeros((256,), jnp.float32)
        return (dense_ctx, ids, tbl_0, tbl_1, tbl_2, tbl_3, tbl_4, tbl_5, tbl_6, tbl_7, tbl_8, tbl_9, tbl_10, tbl_11, tbl_12, tbl_13, tbl_14, tbl_15, tbl_16, tbl_17, tbl_18, tbl_19, tbl_20, tbl_21, tbl_22, tbl_23, tbl_24, tbl_25, tbl_26, tbl_27, tbl_28, tbl_29, tbl_30, tbl_31, tbl_32, tbl_33, tbl_34, tbl_35, tbl_36, tbl_37, tbl_38, W_top1, b_top1, W_top2, b_top2, W_top3)
    dense_ctx, ids, tbl_0, tbl_1, tbl_2, tbl_3, tbl_4, tbl_5, tbl_6, tbl_7, tbl_8, tbl_9, tbl_10, tbl_11, tbl_12, tbl_13, tbl_14, tbl_15, tbl_16, tbl_17, tbl_18, tbl_19, tbl_20, tbl_21, tbl_22, tbl_23, tbl_24, tbl_25, tbl_26, tbl_27, tbl_28, tbl_29, tbl_30, tbl_31, tbl_32, tbl_33, tbl_34, tbl_35, tbl_36, tbl_37, tbl_38, W_top1, b_top1, W_top2, b_top2, W_top3 = _rec_inputs()

    def _L0_rec_setup():
        import jax, jax.numpy as jnp
        import numpy as np
        B, M, D = (1024, 39, 16)
        S1, S2 = (128, 128)

        def _cin_layer(x0, xk, W, b):
            out = jnp.einsum('bhd,bmd,shm->bsd', xk, x0, W) + b[None, :, None]
            return jax.nn.relu(out)
        key = jax.random.key(seed)
        k0, k1, k2 = jax.random.split(key, 3)
        x0 = jax.random.normal(k0, (B, M, D), dtype=jnp.float32)
        W1 = jax.random.normal(k1, (S1, M, M), dtype=jnp.float32) * 0.05
        b1 = jnp.zeros((S1,), dtype=jnp.float32)
        W2 = jax.random.normal(k2, (S2, S1, M), dtype=jnp.float32) * 0.05
        b2 = jnp.zeros((S2,), dtype=jnp.float32)
        return {'x0': x0, 'W1': W1, 'b1': b1, 'W2': W2, 'b2': b2}
    _L0_rec_all = _L0_rec_setup()
    _L0_rec_in = {k: v for k, v in _L0_rec_all.items() if k in ('W1', 'b1', 'W2', 'b2')}
    del _L0_rec_all
    return {'dense_ctx': dense_ctx, 'ids': ids, 'tbl_0': tbl_0, 'tbl_1': tbl_1, 'tbl_2': tbl_2, 'tbl_3': tbl_3, 'tbl_4': tbl_4, 'tbl_5': tbl_5, 'tbl_6': tbl_6, 'tbl_7': tbl_7, 'tbl_8': tbl_8, 'tbl_9': tbl_9, 'tbl_10': tbl_10, 'tbl_11': tbl_11, 'tbl_12': tbl_12, 'tbl_13': tbl_13, 'tbl_14': tbl_14, 'tbl_15': tbl_15, 'tbl_16': tbl_16, 'tbl_17': tbl_17, 'tbl_18': tbl_18, 'tbl_19': tbl_19, 'tbl_20': tbl_20, 'tbl_21': tbl_21, 'tbl_22': tbl_22, 'tbl_23': tbl_23, 'tbl_24': tbl_24, 'tbl_25': tbl_25, 'tbl_26': tbl_26, 'tbl_27': tbl_27, 'tbl_28': tbl_28, 'tbl_29': tbl_29, 'tbl_30': tbl_30, 'tbl_31': tbl_31, 'tbl_32': tbl_32, 'tbl_33': tbl_33, 'tbl_34': tbl_34, 'tbl_35': tbl_35, 'tbl_36': tbl_36, 'tbl_37': tbl_37, 'tbl_38': tbl_38, 'W_top1': W_top1, 'b_top1': b_top1, 'W_top2': W_top2, 'b_top2': b_top2, 'W_top3': W_top3, 'L0_rec_W1': _L0_rec_in['W1'], 'L0_rec_b1': _L0_rec_in['b1'], 'L0_rec_W2': _L0_rec_in['W2'], 'L0_rec_b2': _L0_rec_in['b2']}

def reference(dense_ctx, ids, tbl_0, tbl_1, tbl_2, tbl_3, tbl_4, tbl_5, tbl_6, tbl_7, tbl_8, tbl_9, tbl_10, tbl_11, tbl_12, tbl_13, tbl_14, tbl_15, tbl_16, tbl_17, tbl_18, tbl_19, tbl_20, tbl_21, tbl_22, tbl_23, tbl_24, tbl_25, tbl_26, tbl_27, tbl_28, tbl_29, tbl_30, tbl_31, tbl_32, tbl_33, tbl_34, tbl_35, tbl_36, tbl_37, tbl_38, W_top1, b_top1, W_top2, b_top2, W_top3, L0_rec_W1, L0_rec_b1, L0_rec_W2, L0_rec_b2):
    import jax
    import jax.numpy as jnp

    def _L0_rec_ref(x0, W1, b1, W2, b2):
        import jax, jax.numpy as jnp
        import numpy as np
        B, M, D = (1024, 39, 16)
        S1, S2 = (128, 128)

        def _cin_layer(x0, xk, W, b):
            out = jnp.einsum('bhd,bmd,shm->bsd', xk, x0, W) + b[None, :, None]
            return jax.nn.relu(out)
        x1 = _cin_layer(x0, x0, W1, b1)
        x2 = _cin_layer(x0, x1, W2, b2)
        p1 = x1.sum(axis=-1)
        p2 = x2.sum(axis=-1)
        return jnp.concatenate([p1, p2], axis=-1)
    e = jnp.stack([tbl_0[ids[:, 0]], tbl_1[ids[:, 1]], tbl_2[ids[:, 2]], tbl_3[ids[:, 3]], tbl_4[ids[:, 4]], tbl_5[ids[:, 5]], tbl_6[ids[:, 6]], tbl_7[ids[:, 7]], tbl_8[ids[:, 8]], tbl_9[ids[:, 9]], tbl_10[ids[:, 10]], tbl_11[ids[:, 11]], tbl_12[ids[:, 12]], tbl_13[ids[:, 13]], tbl_14[ids[:, 14]], tbl_15[ids[:, 15]], tbl_16[ids[:, 16]], tbl_17[ids[:, 17]], tbl_18[ids[:, 18]], tbl_19[ids[:, 19]], tbl_20[ids[:, 20]], tbl_21[ids[:, 21]], tbl_22[ids[:, 22]], tbl_23[ids[:, 23]], tbl_24[ids[:, 24]], tbl_25[ids[:, 25]], tbl_26[ids[:, 26]], tbl_27[ids[:, 27]], tbl_28[ids[:, 28]], tbl_29[ids[:, 29]], tbl_30[ids[:, 30]], tbl_31[ids[:, 31]], tbl_32[ids[:, 32]], tbl_33[ids[:, 33]], tbl_34[ids[:, 34]], tbl_35[ids[:, 35]], tbl_36[ids[:, 36]], tbl_37[ids[:, 37]], tbl_38[ids[:, 38]]], axis=1)
    z = _L0_rec_ref(e, L0_rec_W1, L0_rec_b1, L0_rec_W2, L0_rec_b2)
    z = z.reshape(z.shape[0], -1)
    h = jnp.concatenate([z, dense_ctx], axis=1)
    h = jnp.maximum(h @ W_top1 + b_top1, 0.0)
    h = jnp.maximum(h @ W_top2 + b_top2, 0.0)
    y = h @ W_top3
    return y

_drawn_inputs = setup_inputs


def setup_inputs(seed=0):
    import zlib

    import numpy as np

    out = dict(_drawn_inputs(seed))
    spreads = {'b_top1': (0.0, 0.1),
     'b_top2': (0.0, 0.1),
     'L0_rec_b1': (0.0, 0.1),
     'L0_rec_b2': (0.0, 0.1)}
    factors = {'tbl_0': 4.571,
     'tbl_1': 4.281,
     'tbl_2': 7.223,
     'tbl_3': 6.215,
     'tbl_4': 6.502,
     'tbl_5': 7.473,
     'tbl_6': 5.643,
     'tbl_7': 4.392,
     'tbl_8': 8.0,
     'tbl_9': 7.545,
     'tbl_10': 6.249,
     'tbl_11': 5.611,
     'tbl_12': 5.449,
     'tbl_14': 7.879,
     'tbl_15': 6.663,
     'tbl_16': 7.255,
     'tbl_17': 4.614,
     'tbl_18': 5.481,
     'tbl_19': 4.418,
     'tbl_20': 8.0,
     'tbl_21': 3.322,
     'tbl_22': 7.948,
     'tbl_23': 7.291,
     'tbl_24': 8.0,
     'tbl_25': 4.937,
     'tbl_26': 4.276,
     'tbl_27': 6.695,
     'tbl_28': 8.0,
     'tbl_29': 5.196,
     'tbl_30': 5.084,
     'tbl_31': 3.012,
     'tbl_32': 7.83,
     'tbl_33': 7.627,
     'tbl_34': 7.222,
     'tbl_35': 7.011,
     'tbl_36': 8.0,
     'tbl_37': 8.0,
     'tbl_38': 6.17,
     'tbl_13': 4.027}
    for name, (base, spread) in spreads.items():
        noise = np.random.default_rng([zlib.crc32(name.encode()), seed]).standard_normal(out[name].shape)
        drawn = base * np.exp(spread * noise) if base else spread * noise
        out[name] = jnp.asarray(drawn.astype(out[name].dtype))
    for name, factor in factors.items():
        out[name] = (out[name] * factor).astype(out[name].dtype)
    return out
```

```python
import concourse.bass as bass
from concourse import mybir
from contextlib import ExitStack

BATCH = 2048
FIELDS = 39
DIM = 16
S1 = 128
S2 = 128
DENSE = 16
H1 = 512
H2 = 256

P = 128
TILES = BATCH // P
QUARTERS = 4
QDIMS = DIM // QUARTERS
QCOLS = QDIMS * P
SLABS = QUARTERS * QDIMS

SHIFTS = FIELDS // 2 + 1
PAIRS = SHIFTS * FIELDS
CHUNKS = 7
CHUNK = 112
PIECES = QDIMS
PIECE_SHIFTS = SHIFTS // PIECES
XFIELDS = FIELDS + SHIFTS - 1

GROUP = 4
GROUPS = -(-FIELDS // GROUP)
GROUP_OF = [list(range(GROUP * g, min(GROUP * g + GROUP, FIELDS))) for g in range(GROUPS)]
BANKS = 5
A_GROUPS = list(range(0, GROUPS, 2))
D_GROUPS = list(range(1, GROUPS, 2))
NA = len(A_GROUPS)
D_TERMS = sum(len(GROUP_OF[g]) for g in D_GROUPS)
D_UPTO = {g: sum(len(GROUP_OF[x]) for x in D_GROUPS if x <= g) for g in D_GROUPS}
POOL_ADDS = NA - 1
LANES = GROUP + 2
FOLDS = 5
SLOT_AFTER = {2: 0, 5: 1, 8: 2}
EVAC_AFTER = {2: 0, 6: 1, 8: 2}

FIRST_HALF = 20
LAST_TABLES = FIELDS - FIRST_HALF
HALF_SLABS = SLABS // 2


def pair_rows():
    return [(m, (m + k) % FIELDS) for k in range(SHIFTS) for m in range(FIELDS)]


def chunk_size(c):
    return min(CHUNK, PAIRS - CHUNK * c)


def dlrm_tower(nc, dense_t, ids, tables, w1_a, w1_b, b1, w2_t, b2, wt1, bt1, wt2, bt2, wt3, out):
    f32 = mybir.dt.float32
    f32r = mybir.dt.float32r
    i32 = mybir.dt.int32
    ALU = mybir.AluOpType
    ACT = mybir.ActivationFunctionType
    AX = mybir.AxisListType

    ctx = ExitStack()
    with ctx:
        def sb(name, shape, dt=f32):
            return ctx.enter_context(nc.sbuf_tensor(name, shape, dt))

        def sem(name):
            return ctx.enter_context(nc.semaphore(name))

        ids_all = sb("ids_all", [P, TILES + 1, FIELDS], i32)
        idx = sb("idx", [P, FIELDS], i32)
        rows = sb("rows", [P, FIELDS, DIM])
        fields = sb("fields", [P, XFIELDS, DIM])
        act_fields = sb("act_fields", [P, NA, GROUP * DIM])
        dve_fields = sb("dve_fields", [P, FIELDS, DIM])
        pairs = sb("pairs", [P, 2, QDIMS, PAIRS])
        pairs_t = sb("pairs_t", [CHUNK, 2, QCOLS])
        w1 = sb("w1", [CHUNK, CHUNKS, S1])
        w1_other = sb("w1_other", [CHUNK, CHUNKS, S1])
        w2_high = sb("w2_high", [P, FIELDS * S2], f32r)
        w2_low = sb("w2_low", [P, FIELDS * S2], f32r)
        x1_full = sb("x1_full", [P, QCOLS])
        x1_high = sb("x1_high", [P, 2, QCOLS], f32r)
        x1_low = sb("x1_low", [P, 2, QCOLS], f32r)
        scaled = sb("scaled", [P, 2, NA, GROUP * S2])
        lanes = sb("lanes", [P, 2, QDIMS, LANES * S2])
        folded = sb("folded", [P, QDIMS, 3 * S2])
        relu_sum = sb("relu_sum", [P, QDIMS, S2])
        p1_part = sb("p1_part", [P, QUARTERS, P])
        p1_t = sb("p1_t", [P, BATCH])
        p2 = sb("p2", [P, TILES, S2])
        dense_sb = sb("dense_sb", [DENSE, BATCH])
        wt1_sb = sb("wt1_sb", [P, 2, H1])
        wt1_dense = sb("wt1_dense", [DENSE, H1])
        wt2_sb = sb("wt2_sb", [P, H1 // P, H2])
        wt3_sb = sb("wt3_sb", [P, H2 // P])
        b1_sb = sb("b1_sb", [P, 1])
        b2_rows = sb("b2_rows", [P, S2])
        bt1_sb = sb("bt1_sb", [P, H1 // P])
        bt2_sb = sb("bt2_sb", [P, H2 // P])
        ident = sb("ident", [P, P])

        w2_raw = pairs[:].rearrange("p a d n -> p (a d n)")[:, 0:FIELDS * S2]
        h1_sb = pairs[:].rearrange("p a d n -> p (a d n)")[:, 0:2 * (H1 // P) * QCOLS]
        h1_sb = h1_sb.rearrange("p (a c n) -> p a c n", a=2, n=QCOLS)
        after = scaled[:].rearrange("p a g n -> p (a g n)")
        p2_t = after[:, 0:BATCH]
        h2_sb = after[:, BATCH:BATCH + 2 * (H2 // P) * QCOLS].rearrange("p (a c n) -> p a c n", a=2, n=QCOLS)
        y_row = lanes[:].rearrange("p a d n -> p (a d n)")[0:1, 0:BATCH]

        parts = ctx.enter_context(nc.psum_tensor("parts", [P, BANKS, 512], f32))
        turned = ctx.enter_context(nc.psum_tensor("turned", [P, 2, 512], f32))
        x1_sum = ctx.enter_context(nc.psum_tensor("x1_sum", [P, 512], f32))

        ids_loaded = sem("ids_loaded")
        w1_loaded = sem("w1_loaded")
        w2_loaded = sem("w2_loaded")
        top_loaded = sem("top_loaded")
        ident_cleared = sem("ident_cleared")
        ident_made = sem("ident_made")
        w1_made = sem("w1_made")
        w2_high_made = sem("w2_high_made")
        w2_low_made = sem("w2_low_made")
        idx_copied = sem("idx_copied")
        gathered = sem("gathered")
        fields_copied = sem("fields_copied")
        act_fields_copied = sem("act_fields_copied")
        dve_fields_copied = sem("dve_fields_copied")
        pairs_made = sem("pairs_made")
        pairs_turned = sem("pairs_turned")
        pairs_kept = sem("pairs_kept")
        pairs_used = sem("pairs_used")
        x1_full_kept = sem("x1_full_kept")
        x1_high_kept = sem("x1_high_kept")
        x1_low_kept = sem("x1_low_kept")
        p1_part_made = sem("p1_part_made")
        p1_made = sem("p1_made")
        parts_made = sem("parts_made")
        parts_scaled = sem("parts_scaled")
        terms_added = sem("terms_added")
        pool_added = sem("pool_added")
        fold_step = sem("fold_step")
        p2_made = sem("p2_made")
        p2_turned = sem("p2_turned")
        p2_kept = sem("p2_kept")
        h1_made = sem("h1_made")
        h1_kept = sem("h1_kept")
        h2_made = sem("h2_made")
        h2_kept = sem("h2_kept")
        y_made = sem("y_made")
        y_kept = sem("y_kept")
        stored = sem("stored")

        TOP_LOADS = 9
        C1, C2 = H1 // P, H2 // P
        BLOCKS = BATCH // QCOLS

        block = ctx.enter_context(nc.Block())

        @block.sync
        def _(sp):
            sp.dma_start(ids_all[:, 0:1, :], ids[0:P, :].rearrange("(t p) f -> p t f", p=P)).then_inc(ids_loaded, 16)
            sp.dma_start(ids_all[:, 1:TILES, :],
                         ids[P:BATCH, :].rearrange("(t p) f -> p t f", p=P)).then_inc(ids_loaded, 16)
            sp.dma_start(ids_all[:, TILES:TILES + 1, :],
                         ids[0:P, :].rearrange("(t p) f -> p t f", p=P)).then_inc(ids_loaded, 16)
            sp.dma_start(w2_raw, w2_t).then_inc(w2_loaded, 16)
            sp.dma_start(b2_rows[:], bass.AP(tensor=b2.tensor, offset=b2.offset,
                                             ap=[[0, P], [1, S2]])).then_inc(top_loaded, 16)
            sp.dma_start(w1[:], w1_a).then_inc(w1_loaded, 16)
            sp.dma_start(w1_other[:], w1_b).then_inc(w1_loaded, 16)
            sp.dma_start(b1_sb[:], b1).then_inc(top_loaded, 16)
            sp.dma_start(wt1_sb[:], wt1[0:2 * P, :].rearrange("(c p) n -> p c n", p=P)).then_inc(top_loaded, 16)
            sp.dma_start(wt1_dense[:], wt1[2 * P:2 * P + DENSE, :]).then_inc(top_loaded, 16)
            sp.dma_start(wt2_sb[:], wt2.rearrange("(c p) n -> p c n", p=P)).then_inc(top_loaded, 16)
            sp.dma_start(wt3_sb[:], wt3).then_inc(top_loaded, 16)
            sp.dma_start(bt1_sb[:], bt1).then_inc(top_loaded, 16)
            sp.dma_start(bt2_sb[:], bt2).then_inc(top_loaded, 16)
            sp.dma_start(dense_sb[:], dense_t).then_inc(top_loaded, 16)
            sp.wait_ge(y_kept, BLOCKS)
            sp.dma_start(out, y_row).then_inc(stored, 16)
            sp.wait_ge(stored, 16)

        @block.gpsimd
        def _(pool):
            def gather(f, rows_of):
                nc.gpsimd.indirect_dma_start(
                    out=rows[:, f, :], out_offset=None, in_=tables[f],
                    in_offset=bass.IndirectOffsetOnAxis(ap=rows_of[:, f:f + 1], axis=0),
                ).then_inc(gathered, 16)

            pool.wait_ge(ids_loaded, 3 * 16)
            nc.gpsimd.tensor_copy(idx[:], ids_all[:, 0, :]).then_inc(idx_copied, 1)
            pool.wait_ge(idx_copied, 1)
            for f in range(FIELDS):
                gather(f, idx)
            nc.gpsimd.memset(ident[:], 0.0).then_inc(ident_cleared, 1)
            pool.wait_ge(ident_cleared, 1)
            nc.gpsimd.affine_select(out=ident[:], in_=ident[:], compare_op=ALU.not_equal, fill=1.0, base=0,
                                    pattern=[[-1, P]], channel_multiplier=1).then_inc(ident_made, 1)
            pool.wait_ge(gathered, 16 * FIELDS)
            nc.gpsimd.tensor_copy(idx[:], ids_all[:, 1, :]).then_inc(idx_copied, 1)
            pool.wait_ge(idx_copied, 2)
            pool.wait_ge(fields_copied, 2)
            for f in range(FIRST_HALF):
                gather(f, idx)

            def tile(t, first=False, last=False):
                for q in range(QUARTERS):
                    for d in range(QDIMS):
                        i = QDIMS * q + d
                        n = t * SLABS + i
                        into = lanes[:, q % 2, d, 0:GROUP * S2]
                        if i == HALF_SLABS and not last:
                            pool.wait_ge(gathered, (t + 2) * (16 * FIELDS))
                            nc.gpsimd.tensor_copy(idx[:].unsqueeze(1), ids_all[:, bass.ds(t + 2, 1), :]).then_inc(idx_copied, 1)
                            pool.wait_ge(idx_copied, t + 3)
                            pool.wait_ge(fields_copied, (t + 2) * 2)
                        if not (first and q < 2):
                            pool.wait_ge(fold_step, t * (FOLDS * QUARTERS) + (FOLDS * (q - 2) + 2))
                        for a in range(1, NA):
                            pool.wait_ge(parts_scaled, n * NA + (a + 1))
                            if a > 1:
                                pool.wait_ge(pool_added, n * POOL_ADDS + (a - 1))
                            nc.gpsimd.tensor_tensor(
                                out=into, in0=scaled[:, d % 2, 0, :] if a == 1 else into,
                                in1=scaled[:, d % 2, a, :], op=ALU.add).then_inc(pool_added, 1)
                        if i < HALF_SLABS and not last:
                            for f in range(FIRST_HALF + LAST_TABLES * i // HALF_SLABS,
                                           FIRST_HALF + LAST_TABLES * (i + 1) // HALF_SLABS):
                                gather(f, idx)
                        if i >= HALF_SLABS and not last:
                            j = i - HALF_SLABS
                            for f in range(FIRST_HALF * j // HALF_SLABS, FIRST_HALF * (j + 1) // HALF_SLABS):
                                gather(f, idx)

            tile(0, first=True)
            with pool.Fori(1, TILES - 1) as t:
                tile(t)
            tile(TILES - 1, last=True)
            pool.wait_ge(gathered, TILES * 16 * FIELDS + 16 * FIRST_HALF)

        @block.scalar
        def _(act):
            def keep_pairs(c, quarter, head=False):
                b = c % 2
                act.wait_ge(pairs_turned, quarter * CHUNKS + (c + 1))
                if c >= 2:
                    act.wait_ge(pairs_used, quarter * CHUNKS + (c - 1))
                elif not head:
                    act.wait_ge(pairs_used, quarter * CHUNKS - c)
                k = chunk_size(c)
                nc.scalar.activation(pairs_t[0:k, b, :], turned[0:k, b, :], ACT.Copy).then_inc(pairs_kept, 1)

            def keep_x1(quarter, parity, nth=None):
                act.wait_ge(pairs_used, quarter * CHUNKS + CHUNKS)
                if nth != 0:
                    act.wait_ge(x1_low_kept, quarter)
                    act.wait_ge(p1_part_made, quarter)
                nc.scalar.activation(x1_full[:], x1_sum[:], ACT.Relu, bias=b1_sb[:, 0:1]).then_inc(x1_full_kept, 1)
                if nth not in (0, 1):
                    act.wait_ge(parts_made, quarter * (GROUPS * QDIMS) - GROUPS * QDIMS)
                nc.scalar.activation(x1_high[:, parity, :], x1_sum[:], ACT.Relu,
                                     bias=b1_sb[:, 0:1]).then_inc(x1_high_kept, 1)

            act.wait_ge(top_loaded, 16 * TOP_LOADS)
            for c in range(CHUNKS):
                keep_pairs(c, 0, head=True)
            keep_x1(0, 0, nth=0)

            def tile(t, first=False, last=False):
                act.wait_ge(fields_copied, t * 2 + 2)
                if not first:
                    act.wait_ge(parts_scaled, t * (NA * SLABS))
                nc.scalar.activation(act_fields[:],
                                     fields[:, 0:2 * GROUP * NA, :].rearrange("p (g w) d -> p g (w d)", g=NA)
                                     [:, :, 0:GROUP * DIM], ACT.Copy).then_inc(act_fields_copied, 1)
                act.wait_ge(act_fields_copied, t + 1)
                for q in range(QUARTERS):
                    more = not (last and q == QUARTERS - 1)
                    for d in range(QDIMS):
                        i = QDIMS * q + d
                        n = t * SLABS + i
                        if not (first and i < 2):
                            act.wait_ge(pool_added, n * POOL_ADDS - POOL_ADDS)
                        for a, g in enumerate(A_GROUPS):
                            act.wait_ge(parts_made, n * GROUPS + (g + 1))
                            for j in range(GROUP):
                                at = DIM * j + i
                                last_one = nc.scalar.activation(
                                    scaled[:, d % 2, a, S2 * j:S2 * (j + 1)],
                                    parts[:, g % BANKS, S2 * j:S2 * (j + 1)], ACT.Copy,
                                    scale=act_fields[:, a, at:at + 1])
                            last_one.then_inc(parts_scaled, 1)
                            if g in EVAC_AFTER and more:
                                c = 3 * d + EVAC_AFTER[g]
                                if c < CHUNKS:
                                    keep_pairs(c, t * QUARTERS + (q + 1))
                        if d == 2 and more:
                            keep_x1(t * QUARTERS + (q + 1), (q + 1) % 2, nth=1 if first and q == 0 else None)

            tile(0, first=True)
            with act.Fori(1, TILES - 1) as t:
                tile(t)
            tile(TILES - 1, last=True)

            def keep_p2(b):
                act.wait_ge(p2_turned, b + 1)
                nc.scalar.activation(p2_t[:, QCOLS * b:QCOLS * (b + 1)], turned[:, b % 2, :],
                                     ACT.Copy).then_inc(p2_kept, 1)

            def keep_h1(b):
                if b >= 2:
                    act.wait_ge(h2_made, C2 * (b - 1))
                for c in range(C1):
                    act.wait_ge(h1_made, C1 * b + c + 1)
                    nc.scalar.activation(h1_sb[:, b % 2, c, :], parts[:, c, :], ACT.Relu,
                                         bias=bt1_sb[:, c:c + 1]).then_inc(h1_kept, 1)

            def keep_h2(b):
                if b >= 2:
                    act.wait_ge(y_made, b - 1)
                for c in range(C2):
                    act.wait_ge(h2_made, C2 * b + c + 1)
                    bank = parts[:, 4, :] if c == 0 else x1_sum[:]
                    nc.scalar.activation(h2_sb[:, b % 2, c, :], bank, ACT.Relu,
                                         bias=bt2_sb[:, c:c + 1]).then_inc(h2_kept, 1)

            def keep_y(b):
                act.wait_ge(y_made, b + 1)
                nc.scalar.activation(y_row[:, QCOLS * b:QCOLS * (b + 1)], turned[0:1, b % 2, :],
                                     ACT.Copy).then_inc(y_kept, 1)

            act.wait_ge(pool_added, TILES * SLABS * POOL_ADDS)
            act.wait_ge(p2_made, TILES)
            for b in range(BLOCKS):
                keep_p2(b)
            for step in range(BLOCKS + 2):
                if step < BLOCKS:
                    keep_h1(step)
                if 0 <= step - 1 < BLOCKS:
                    keep_h2(step - 1)
                if 0 <= step - 2 < BLOCKS:
                    keep_y(step - 2)

        @block.vector
        def _(dve):
            def copy_fields(t, first=False):
                dve.wait_ge(gathered, t * (16 * FIELDS) + 16 * FIELDS)
                if not first:
                    dve.wait_ge(pairs_made, t * (PIECES * QUARTERS))
                    dve.wait_ge(act_fields_copied, t)
                    dve.wait_ge(dve_fields_copied, t)
                nc.vector.tensor_copy(fields[:, 0:FIELDS, :], rows[:]).then_inc(fields_copied, 1)
                nc.vector.tensor_copy(fields[:, FIELDS:XFIELDS, :], rows[:, 0:XFIELDS - FIELDS, :]).then_inc(fields_copied, 1)

            def make_pairs(q, piece):
                k0 = PIECE_SHIFTS * piece
                one = fields[:, 0:FIELDS, QDIMS * q:QDIMS * (q + 1)].unsqueeze(1)
                one = one.broadcast_to([P, PIECE_SHIFTS, FIELDS, QDIMS])
                at = fields[:, k0:XFIELDS, QDIMS * q:QDIMS * (q + 1)]
                other = bass.AP(tensor=at.tensor, offset=at.offset,
                                ap=[list(at.ap[0]), [DIM, PIECE_SHIFTS], [DIM, FIELDS], [1, QDIMS]])
                into = pairs[:, q % 2, :, FIELDS * k0:FIELDS * (k0 + PIECE_SHIFTS)]
                into = into.rearrange("p d (k m) -> p k m d", m=FIELDS)
                nc.vector.tensor_tensor(out=into, in0=one, in1=other, op=ALU.mult).then_inc(pairs_made, 1)

            def split_x1(quarter, parity, part, nth=None):
                dve.wait_ge(x1_full_kept, quarter + 1)
                dve.wait_ge(x1_high_kept, quarter + 1)
                if nth not in (0, 1):
                    dve.wait_ge(parts_made, quarter * (GROUPS * QDIMS) - GROUPS * QDIMS)
                nc.vector.tensor_tensor(out=x1_low[:, parity, :], in0=x1_full[:],
                                        in1=x1_high[:, parity, :].bitcast(f32), op=ALU.subtract).then_inc(x1_low_kept, 1)
                nc.vector.tensor_reduce(out=p1_part[:, part, :], in_=x1_full[:].rearrange("p (d b) -> p b d", d=QDIMS),
                                        op=ALU.add, axis=AX.X).then_inc(p1_part_made, 1)

            def fold(step, t, q):
                base = t * (FOLDS * QUARTERS) + FOLDS * q
                if step < 2:
                    d0 = 2 * step
                    dve.wait_ge(pool_added, t * (POOL_ADDS * SLABS) + POOL_ADDS * (QDIMS * q + d0 + 2))
                    dve.wait_ge(terms_added, t * (D_TERMS * SLABS) + D_TERMS * (QDIMS * q + d0 + 2))
                    nc.vector.tensor_tensor(out=folded[:, d0:d0 + 2, :], in0=lanes[:, q % 2, d0:d0 + 2, 0:3 * S2],
                                            in1=lanes[:, q % 2, d0:d0 + 2, 3 * S2:6 * S2],
                                            op=ALU.add).then_inc(fold_step, 1)
                elif step < 4:
                    dve.wait_ge(fold_step, base + step)
                    nc.vector.tensor_tensor(out=folded[:, :, 0:S2], in0=folded[:, :, 0:S2],
                                            in1=folded[:, :, S2 * (step - 1):S2 * step],
                                            op=ALU.add).then_inc(fold_step, 1)
                else:
                    dve.wait_ge(fold_step, base + step)
                    if q == 0:
                        nc.vector.tensor_scalar(out=relu_sum[:], in0=folded[:, :, 0:S2], scalar1=0.0, scalar2=None,
                                                op0=ALU.max).then_inc(fold_step, 1)
                    else:
                        nc.vector.scalar_tensor_tensor(out=relu_sum[:], in0=folded[:, :, 0:S2], scalar=0.0,
                                                       in1=relu_sum[:], op0=ALU.max, op1=ALU.add).then_inc(fold_step, 1)

            def keep_p2(t):
                dve.wait_ge(fold_step, t * (FOLDS * QUARTERS) + FOLDS * QUARTERS)
                nc.vector.tensor_reduce(out=p2[:, bass.ds(t, 1), :].rearrange("p a s -> p (a s)"),
                                        in_=relu_sum[:].rearrange("p d s -> p s d"),
                                        op=ALU.add, axis=AX.X).then_inc(p2_made, 1)

            dve.wait_ge(w2_loaded, 16)
            nc.vector.tensor_copy(w2_high[:], w2_raw).then_inc(w2_high_made, 1)
            dve.wait_ge(w2_high_made, 1)
            nc.vector.tensor_tensor(out=w2_low[:], in0=w2_raw, in1=w2_high[:].bitcast(f32),
                                    op=ALU.subtract).then_inc(w2_low_made, 1)
            dve.wait_ge(w1_loaded, 32)
            nc.vector.tensor_tensor(out=w1[:], in0=w1[:], in1=w1_other[:], op=ALU.add).then_inc(w1_made, 1)

            copy_fields(0, first=True)
            dve.wait_ge(fields_copied, 2)
            dve.wait_ge(w2_low_made, 1)
            for q in range(2):
                for piece in range(PIECES):
                    make_pairs(q, piece)
            dve.wait_ge(top_loaded, 16 * TOP_LOADS)
            split_x1(0, 0, 0, nth=0)

            def tile(t, first=False, last=False):
                if not first:
                    dve.wait_ge(terms_added, t * (D_TERMS * SLABS))
                nc.vector.tensor_copy(dve_fields[:], fields[:, 0:FIELDS, :]).then_inc(dve_fields_copied, 1)
                dve.wait_ge(dve_fields_copied, t + 1)
                for q in range(QUARTERS):
                    quarter = t * QUARTERS + q
                    for d in range(QDIMS):
                        i = QDIMS * q + d
                        n = t * SLABS + i
                        made = 0
                        for g in D_GROUPS:
                            dve.wait_ge(parts_made, n * GROUPS + (g + 1))
                            for j, m in enumerate(GROUP_OF[g]):
                                into = lanes[:, q % 2, d, S2 * (GROUP + made % 2):S2 * (GROUP + made % 2 + 1)]
                                part = parts[:, g % BANKS, S2 * j:S2 * (j + 1)]
                                scale = dve_fields[:, m, i:i + 1]
                                if made == 1:
                                    nc.vector.tensor_scalar(out=into, in0=part, scalar1=scale, scalar2=None,
                                                            op0=ALU.mult).then_inc(terms_added, 1)
                                else:
                                    if made:
                                        dve.wait_ge(terms_added, n * D_TERMS + (made - 1))
                                    nc.vector.scalar_tensor_tensor(
                                        out=into, in0=part, scalar=scale, in1=into if made else b2_rows[:],
                                        op0=ALU.mult, op1=ALU.add).then_inc(terms_added, 1)
                                made += 1
                            if g == 1 and d == 3 and not (last and q == QUARTERS - 1):
                                split_x1(t * QUARTERS + (q + 1), (q + 1) % 2, (q + 1) % QUARTERS,
                                         nth=1 if first and q == 0 else None)
                            if g == 1 and q == 3 and d == 1:
                                dve.wait_ge(p1_part_made, t * QUARTERS + QUARTERS)
                                nc.vector.tensor_reduce(out=p1_t[:, bass.ds(t * P, P)],
                                                        in_=p1_part[:].rearrange("p q b -> p b q"),
                                                        op=ALU.add, axis=AX.X).then_inc(p1_made, 1)
                            if g == 3 and q == 2 and d == 0 and not last:
                                copy_fields(t + 1)
                            if g == 5 and not (last and q >= 2):
                                if q >= 2 and d == 0:
                                    dve.wait_ge(fields_copied, (t + 2) * 2)
                                if d == 0:
                                    dve.wait_ge(pairs_turned, quarter * CHUNKS + CHUNKS)
                                make_pairs((q + 2) % QUARTERS, d)
                            if g == 7 and not (first and q == 0):
                                before = (t, q - 1) if q else (t - 1, QUARTERS - 1)
                                if d == 1:
                                    fold(0, *before)
                                elif d == 2:
                                    fold(1, *before)
                            if d == 3 and not (first and q == 0):
                                before = (t, q - 1) if q else (t - 1, QUARTERS - 1)
                                if g in (3, 5, 7):
                                    fold({3: 2, 5: 3, 7: 4}[g], *before)
                            if g == 1 and q == 1 and d == 0 and not first:
                                keep_p2(t - 1)

            tile(0, first=True)
            with dve.Fori(1, TILES - 1) as t:
                tile(t)
            tile(TILES - 1, last=True)
            for step in range(FOLDS):
                fold(step, TILES - 1, QUARTERS - 1)
            keep_p2(TILES - 1)

        @block.tensor
        def _(pe):
            def turn_pairs(c, quarter, parity, head=False):
                b = c % 2
                pieces = min(PIECES, -(-(CHUNK * (c + 1)) // (FIELDS * PIECE_SHIFTS)))
                pe.wait_ge(pairs_made, quarter * PIECES + pieces)
                if c >= 2:
                    pe.wait_ge(pairs_kept, quarter * CHUNKS + (c - 1))
                elif not head:
                    pe.wait_ge(pairs_kept, quarter * CHUNKS - c)
                k = chunk_size(c)
                for d in range(QDIMS):
                    last_one = nc.tensor.transpose(turned[0:k, b, P * d:P * (d + 1)],
                                                   pairs[:, parity, d, CHUNK * c:CHUNK * c + k], ident[:])
                last_one.then_inc(pairs_turned, 1)

            def use_pairs(c, quarter, head=False):
                k = chunk_size(c)
                pe.wait_ge(pairs_kept, quarter * CHUNKS + (c + 1))
                if c == 0 and not head:
                    pe.wait_ge(x1_high_kept, quarter)
                nc.tensor.matmul(x1_sum[:], w1[0:k, c, :], pairs_t[0:k, c % 2, :],
                                 start=(c == 0), stop=(c == CHUNKS - 1)).then_inc(pairs_used, 1)

            pe.wait_ge(ident_made, 1)
            pe.wait_ge(w1_made, 1)
            for slot in range(CHUNKS + 1):
                if slot < CHUNKS:
                    turn_pairs(slot, 0, 0, head=True)
                if slot:
                    use_pairs(slot - 1, 0, head=True)
            pe.wait_ge(w2_low_made, 1)

            def tile(t, first=False, last=False):
                for q in range(QUARTERS):
                    quarter = t * QUARTERS + q
                    more = not (last and q == QUARTERS - 1)
                    pe.wait_ge(x1_high_kept, quarter + 1)
                    pe.wait_ge(x1_low_kept, quarter + 1)
                    for d in range(QDIMS):
                        i = QDIMS * q + d
                        n = t * SLABS + i
                        high = x1_high[:, q % 2, P * d:P * (d + 1)]
                        low = x1_low[:, q % 2, P * d:P * (d + 1)]
                        for g in range(GROUPS):
                            if not (first and i == 0 and g < BANKS):
                                was = g - BANKS if g >= BANKS else g - BANKS + GROUPS
                                slab = n if g >= BANKS else n - 1
                                if was % 2 == 0:
                                    pe.wait_ge(parts_scaled, slab * NA + (was // 2 + 1))
                                else:
                                    pe.wait_ge(terms_added, slab * D_TERMS + D_UPTO[was])
                            m = GROUP_OF[g]
                            w = slice(S2 * m[0], S2 * (m[-1] + 1))
                            into = parts[:, g % BANKS, 0:S2 * len(m)]
                            nc.tensor.matmul(into, high, w2_high[:, w], start=True, stop=False)
                            nc.tensor.matmul(into, high, w2_low[:, w], start=False, stop=False)
                            nc.tensor.matmul(into, low, w2_high[:, w], start=False, stop=True).then_inc(parts_made, 1)
                            slot = 3 * d + SLOT_AFTER.get(g, CHUNKS)
                            if g in SLOT_AFTER and slot <= CHUNKS and more:
                                if slot:
                                    use_pairs(slot - 1, t * QUARTERS + (q + 1))
                                if slot < CHUNKS:
                                    turn_pairs(slot, t * QUARTERS + (q + 1), (q + 1) % 2)

            tile(0, first=True)
            with pe.Fori(1, TILES - 1) as t:
                tile(t)
            tile(TILES - 1, last=True)

            pe.wait_ge(top_loaded, 16 * TOP_LOADS)
            pe.wait_ge(p1_made, TILES)
            pe.wait_ge(p2_made, TILES)

            def turn_p2(b):
                if b >= 2:
                    pe.wait_ge(p2_kept, b - 1)
                for j in range(QCOLS // P):
                    last_one = nc.tensor.transpose(turned[:, b % 2, P * j:P * (j + 1)],
                                                   p2[:, QCOLS // P * b + j, :], ident[:])
                last_one.then_inc(p2_turned, 1)

            def make_h1(b):
                cols = slice(QCOLS * b, QCOLS * (b + 1))
                pe.wait_ge(p2_kept, b + 1)
                for c in range(C1):
                    if b:
                        pe.wait_ge(h1_kept, C1 * (b - 1) + c + 1)
                    o = slice(P * c, P * (c + 1))
                    nc.tensor.matmul(parts[:, c, :], wt1_sb[:, 0, o], p1_t[:, cols], start=True, stop=False)
                    nc.tensor.matmul(parts[:, c, :], wt1_sb[:, 1, o], p2_t[:, cols], start=False, stop=False)
                    nc.tensor.matmul(parts[:, c, :], wt1_dense[:, o], dense_sb[:, cols],
                                     start=False, stop=True).then_inc(h1_made, 1)

            def make_h2(b):
                for c in range(C2):
                    if b:
                        pe.wait_ge(h2_kept, C2 * (b - 1) + c + 1)
                    bank = parts[:, 4, :] if c == 0 else x1_sum[:]
                    for k in range(C1):
                        pe.wait_ge(h1_kept, C1 * b + k + 1)
                        last_one = nc.tensor.matmul(bank, wt2_sb[:, k, P * c:P * (c + 1)], h1_sb[:, b % 2, k, :],
                                                    start=(k == 0), stop=(k == C1 - 1))
                    last_one.then_inc(h2_made, 1)

            def make_y(b):
                pe.wait_ge(p2_kept, BLOCKS)
                if b >= 2:
                    pe.wait_ge(y_kept, b - 1)
                for k in range(C2):
                    pe.wait_ge(h2_kept, C2 * b + k + 1)
                    last_one = nc.tensor.matmul(turned[0:1, b % 2, :], wt3_sb[:, k:k + 1], h2_sb[:, b % 2, k, :],
                                                start=(k == 0), stop=(k == C2 - 1))
                last_one.then_inc(y_made, 1)

            for b in range(BLOCKS):
                turn_p2(b)
            for step in range(BLOCKS + 2):
                if step < BLOCKS:
                    make_h1(step)
                if 0 <= step - 1 < BLOCKS:
                    make_h2(step - 1)
                if 0 <= step - 2 < BLOCKS:
                    make_y(step - 2)


def kernel(**inputs):
    import numpy as np
    import concourse.bacc as bacc
    from concourse.bass_utils import run_bass_kernel_spmd

    nc = bacc.Bacc("TRN2", target_bir_lowering=False, num_devices=1)
    arrays = {}

    def given(name, a):
        a = np.ascontiguousarray(a)
        arrays[name] = a
        return nc.dram_tensor(name, a.shape, mybir.dt.from_np(a.dtype), kind="ExternalInput").ap()

    W1 = np.asarray(inputs["L0_rec_W1"])
    firsts, seconds = (list(x) for x in zip(*pair_rows()))
    w1_a = np.zeros((CHUNK * CHUNKS, S1), W1.dtype)
    w1_b = np.zeros((CHUNK * CHUNKS, S1), W1.dtype)
    w1_a[0:PAIRS] = W1[:, firsts, seconds].T
    w1_b[FIELDS:PAIRS] = W1[:, seconds[FIELDS:], firsts[FIELDS:]].T

    def by_chunk(w):
        return w.reshape(CHUNKS, CHUNK, S1).transpose(1, 0, 2)

    W2 = np.asarray(inputs["L0_rec_W2"])
    args = [
        given("dense_t", np.asarray(inputs["dense_ctx"]).T),
        given("ids", np.asarray(inputs["ids"])),
        [given(f"tbl_{f}", np.asarray(inputs[f"tbl_{f}"])) for f in range(FIELDS)],
        given("w1_a", by_chunk(w1_a)),
        given("w1_b", by_chunk(w1_b)),
        given("b1", np.asarray(inputs["L0_rec_b1"]).reshape(S1, 1)),
        given("w2_t", W2.transpose(1, 2, 0).reshape(S1, FIELDS * S2)),
        given("b2", np.asarray(inputs["L0_rec_b2"])),
        given("wt1", np.asarray(inputs["W_top1"])),
        given("bt1", np.asarray(inputs["b_top1"]).reshape(H1 // P, P).T),
        given("wt2", np.asarray(inputs["W_top2"])),
        given("bt2", np.asarray(inputs["b_top2"]).reshape(H2 // P, P).T),
        given("wt3", np.asarray(inputs["W_top3"]).reshape(H2 // P, P).T),
    ]
    out = nc.dram_tensor("y", (1, BATCH), mybir.dt.float32, kind="ExternalOutput").ap()
    dlrm_tower(nc, *args, out)
    r = run_bass_kernel_spmd(nc, [arrays], core_ids=[0])
    return r.results[0]["y"].reshape(BATCH, 1)
```

```python
import concourse.bass as bass
from concourse import mybir
from contextlib import ExitStack

BATCH = 2048
FIELDS = 39
DIM = 16
S1 = 128
S2 = 128
DENSE = 16
H1 = 512
H2 = 256

P = 128
TILES = BATCH // P
QUARTERS = 4
QDIMS = DIM // QUARTERS
QCOLS = QDIMS * P
SLABS = QUARTERS * QDIMS

SHIFTS = FIELDS // 2 + 1
PAIRS = SHIFTS * FIELDS
CHUNK_SHIFTS = 3
CHUNKS = -(-SHIFTS // CHUNK_SHIFTS)
CHUNK = CHUNK_SHIFTS * FIELDS
XFIELDS = 2 * FIELDS

GROUP = 4
GROUPS = -(-FIELDS // GROUP)
GROUP_OF = [list(range(GROUP * g, min(GROUP * g + GROUP, FIELDS))) for g in range(GROUPS)]
BANKS = 5
A_GROUPS = list(range(0, GROUPS, 2))
D_GROUPS = list(range(1, GROUPS, 2))
NA = len(A_GROUPS)
D_TERMS = sum(len(GROUP_OF[g]) for g in D_GROUPS)
D_UPTO = {g: sum(len(GROUP_OF[x]) for x in D_GROUPS if x <= g) for g in D_GROUPS}
POOL_ADDS = NA - 1
LANES = GROUP + 2
FOLDS = 5
SLOTS = 4

FIELDS_AT = (2, 3)
TURN_AT = (2, 9)
KEEP_AT = (3, 0)
PAIRS_AT = {(1, 7): (2, 0), (2, 1): (2, 1), (2, 5): (2, 2), (2, 9): (2, 3),
            (3, 3): (2, 4), (3, 7): (2, 5), (0, 3): (1, 6)}
USE_AT = {(2, 3): (2, 0), (2, 8): (2, 1), (3, 3): (2, 2), (3, 8): (2, 3),
          (0, 2): (1, 4), (0, 7): (1, 5), (1, 2): (1, 6)}
FIRST_PAIRS_AT = {(0, 1): (1, 0), (0, 3): (1, 1), (0, 5): (1, 2), (0, 7): (1, 3),
                  (0, 9): (1, 4), (1, 1): (1, 5), (1, 3): (1, 6)}
FIRST_USE_AT = {(0, 3): (1, 0), (0, 5): (1, 1), (0, 7): (1, 2), (0, 9): (1, 3),
                (1, 1): (1, 4), (1, 3): (1, 5), (1, 5): (1, 6)}
X1_AT = (1, 4)
SPLIT_AT = (3, 5)
FOLD_AT = {(0, 5): 0, (1, 1): 1, (1, 3): 2, (1, 5): 3, (2, 1): 4}
P1_AT = (2, 7)
P2_AT = (3, 9)
AHEAD = 3

GATHER_SLAB = 6
FIRST_TABLES = 26
LAST_SLAB = 5
LAST_TABLES = FIELDS - FIRST_TABLES
LATE_SLABS = SLABS - GATHER_SLAB


def chunk_at(places, first_places, here, first_quarter):
    if not first_quarter:
        return places.get(here)
    two_ahead = {at: what for at, what in places.items() if what[0] == 2}
    return {**two_ahead, **first_places}.get(here)


def pair_rows():
    return [(m, (m + k) % FIELDS) for k in range(SHIFTS) for m in range(FIELDS)]


def chunk_shifts(c):
    return range(CHUNK_SHIFTS * c, min(CHUNK_SHIFTS * (c + 1), SHIFTS))


def chunk_size(c):
    return FIELDS * len(chunk_shifts(c))


def dlrm_tower(nc, dense_t, ids, tables, w1_a, w1_b, b1, w2_t, b2, wt1, bt1, wt2, bt2, wt3, out):
    f32 = mybir.dt.float32
    f32r = mybir.dt.float32r
    i32 = mybir.dt.int32
    ALU = mybir.AluOpType
    ACT = mybir.ActivationFunctionType
    AX = mybir.AxisListType

    ctx = ExitStack()
    with ctx:
        def sb(name, shape, dt=f32):
            return ctx.enter_context(nc.sbuf_tensor(name, shape, dt))

        def sem(name):
            return ctx.enter_context(nc.semaphore(name))

        ids_all = sb("ids_all", [P, TILES + 1, FIELDS], i32)
        idx = sb("idx", [P, FIELDS], i32)
        rows = sb("rows", [P, FIELDS, DIM])
        fields = sb("fields", [P, XFIELDS, DIM])
        act_fields = sb("act_fields", [P, NA, GROUP * DIM])
        dve_fields = sb("dve_fields", [P, FIELDS, DIM])
        fields_t = sb("fields_t", [XFIELDS, 2, QCOLS])
        one = sb("one", [P, 2, QCOLS])
        other = sb("other", [P, 2, CHUNKS, QCOLS])
        pairs = sb("pairs", [CHUNK, CHUNKS, QCOLS])
        w1 = sb("w1", [CHUNK, CHUNKS, S1])
        w2_high = sb("w2_high", [P, FIELDS * S2], f32r)
        w2_low = sb("w2_low", [P, FIELDS * S2], f32r)
        x1_full = sb("x1_full", [P, QCOLS])
        x1_high = sb("x1_high", [P, 2, QCOLS], f32r)
        x1_low = sb("x1_low", [P, 2, QCOLS], f32r)
        scaled = sb("scaled", [P, 2, NA, GROUP * S2])
        lanes = sb("lanes", [P, 2, QDIMS, LANES * S2])
        folded = sb("folded", [P, QDIMS, 3 * S2])
        relu_sum = sb("relu_sum", [P, QDIMS, S2])
        p1_part = sb("p1_part", [P, QUARTERS, P])
        p1_t = sb("p1_t", [P, BATCH])
        p2 = sb("p2", [P, TILES, S2])
        dense_sb = sb("dense_sb", [DENSE, BATCH])
        wt1_sb = sb("wt1_sb", [P, 2, H1])
        wt1_dense = sb("wt1_dense", [DENSE, H1])
        wt2_sb = sb("wt2_sb", [P, H1 // P, H2])
        wt3_sb = sb("wt3_sb", [P, H2 // P])
        b1_sb = sb("b1_sb", [P, 1])
        b2_rows = sb("b2_rows", [P, S2])
        bt1_sb = sb("bt1_sb", [P, H1 // P])
        bt2_sb = sb("bt2_sb", [P, H2 // P])
        ident = sb("ident", [P, P])

        w2_raw = other[:].rearrange("p a c n -> p (a c n)")[:, 0:FIELDS * S2]
        h1_sb = other[:].rearrange("p a c n -> p (a c n)")[:, 0:2 * (H1 // P) * QCOLS]
        h1_sb = h1_sb.rearrange("p (a c n) -> p a c n", a=2, n=QCOLS)
        after = scaled[:].rearrange("p a g n -> p (a g n)")
        w1_other = after[0:CHUNK, 0:CHUNKS * S1].rearrange("p (c s) -> p c s", s=S1)
        p2_t = other[:].rearrange("p a c n -> p (a c n)")[:, 2 * (H1 // P) * QCOLS:2 * (H1 // P) * QCOLS + BATCH]
        h2_sb = after[:, 0:2 * (H2 // P) * QCOLS].rearrange("p (a c n) -> p a c n", a=2, n=QCOLS)
        y_row = lanes[:].rearrange("p a d n -> p (a d n)")[0:1, 0:BATCH]

        parts = ctx.enter_context(nc.psum_tensor("parts", [P, BANKS, 512], f32))
        turned = ctx.enter_context(nc.psum_tensor("turned", [P, 2, 512], f32))
        x1_sum = ctx.enter_context(nc.psum_tensor("x1_sum", [P, 512], f32))

        ids_loaded = sem("ids_loaded")
        w1_loaded = sem("w1_loaded")
        w2_loaded = sem("w2_loaded")
        top_loaded = sem("top_loaded")
        ident_cleared = sem("ident_cleared")
        ident_made = sem("ident_made")
        w1_made = sem("w1_made")
        w2_high_made = sem("w2_high_made")
        w2_low_made = sem("w2_low_made")
        idx_copied = sem("idx_copied")
        gathered = sem("gathered")
        fields_copied = sem("fields_copied")
        act_fields_copied = sem("act_fields_copied")
        dve_fields_copied = sem("dve_fields_copied")
        fields_turned = sem("fields_turned")
        fields_t_kept = sem("fields_t_kept")
        one_spread = [sem(f"one_spread_{p}") for p in range(2)]
        other_spread = [[sem(f"other_spread_{p}_{c}") for c in range(CHUNKS)] for p in range(2)]
        pairs_made = sem("pairs_made")
        pairs_used = sem("pairs_used")
        x1_full_kept = sem("x1_full_kept")
        x1_high_kept = sem("x1_high_kept")
        x1_low_kept = sem("x1_low_kept")
        p1_part_made = sem("p1_part_made")
        p1_made = sem("p1_made")
        parts_made = sem("parts_made")
        parts_scaled = sem("parts_scaled")
        terms_added = sem("terms_added")
        pool_added = sem("pool_added")
        fold_step = sem("fold_step")
        p2_made = sem("p2_made")
        p2_turned = sem("p2_turned")
        p2_kept = sem("p2_kept")
        h1_made = sem("h1_made")
        h1_kept = sem("h1_kept")
        h2_made = sem("h2_made")
        h2_kept = sem("h2_kept")
        y_made = sem("y_made")
        y_kept = sem("y_kept")
        stored = sem("stored")

        TOP_LOADS = 9
        C1, C2 = H1 // P, H2 // P
        BLOCKS = BATCH // QCOLS

        block = ctx.enter_context(nc.Block())

        @block.sync
        def _(sp):
            sp.dma_start(ids_all[:, 0:1, :], ids[0:P, :].rearrange("(t p) f -> p t f", p=P)).then_inc(ids_loaded, 16)
            sp.dma_start(ids_all[:, 1:TILES, :],
                         ids[P:BATCH, :].rearrange("(t p) f -> p t f", p=P)).then_inc(ids_loaded, 16)
            sp.dma_start(ids_all[:, TILES:TILES + 1, :],
                         ids[0:P, :].rearrange("(t p) f -> p t f", p=P)).then_inc(ids_loaded, 16)
            sp.dma_start(w2_raw, w2_t).then_inc(w2_loaded, 16)
            sp.dma_start(b2_rows[:], bass.AP(tensor=b2.tensor, offset=b2.offset,
                                             ap=[[0, P], [1, S2]])).then_inc(top_loaded, 16)
            sp.dma_start(w1[:], w1_a).then_inc(w1_loaded, 16)
            sp.dma_start(w1_other, w1_b).then_inc(w1_loaded, 16)
            sp.dma_start(b1_sb[:], b1).then_inc(top_loaded, 16)
            sp.dma_start(wt1_sb[:], wt1[0:2 * P, :].rearrange("(c p) n -> p c n", p=P)).then_inc(top_loaded, 16)
            sp.dma_start(wt1_dense[:], wt1[2 * P:2 * P + DENSE, :]).then_inc(top_loaded, 16)
            sp.dma_start(wt2_sb[:], wt2.rearrange("(c p) n -> p c n", p=P)).then_inc(top_loaded, 16)
            sp.dma_start(wt3_sb[:], wt3).then_inc(top_loaded, 16)
            sp.dma_start(bt1_sb[:], bt1).then_inc(top_loaded, 16)
            sp.dma_start(bt2_sb[:], bt2).then_inc(top_loaded, 16)
            sp.dma_start(dense_sb[:], dense_t).then_inc(top_loaded, 16)

            def spread_fields(t, q, head=False):
                sp.wait_ge(fields_t_kept, t * QUARTERS + (q + 1))
                if head:
                    sp.wait_ge(w2_low_made, 1)
                p = q % 2
                for i in range(CHUNK_SHIFTS):
                    sp.dma_start(one[FIELDS * i:FIELDS * (i + 1), p, :], fields_t[0:FIELDS, p, :]).then_inc(one_spread[p], 16)
                for c in range(CHUNKS):
                    for i, k in enumerate(chunk_shifts(c)):
                        sp.dma_start(other[FIELDS * i:FIELDS * (i + 1), p, c, :],
                                     fields_t[k:k + FIELDS, p, :]).then_inc(other_spread[p][c], 16)

            for quarter in range(AHEAD):
                spread_fields(0, quarter, head=quarter == 0)

            def tile(t, last=False):
                for q in range(QUARTERS):
                    if not (last and q + AHEAD >= QUARTERS):
                        spread_fields(t + (q + AHEAD) // QUARTERS, (q + AHEAD) % QUARTERS)

            with sp.Fori(0, TILES - 1) as t:
                tile(t)
            tile(TILES - 1, last=True)
            sp.wait_ge(y_kept, BLOCKS)
            sp.dma_start(out, y_row).then_inc(stored, 16)
            sp.wait_ge(stored, 16)

        @block.gpsimd
        def _(pool):
            def gather(f, rows_of):
                nc.gpsimd.indirect_dma_start(
                    out=rows[:, f, :], out_offset=None, in_=tables[f],
                    in_offset=bass.IndirectOffsetOnAxis(ap=rows_of[:, f:f + 1], axis=0),
                ).then_inc(gathered, 16)

            pool.wait_ge(ids_loaded, 3 * 16)
            nc.gpsimd.tensor_copy(idx[:], ids_all[:, 0, :]).then_inc(idx_copied, 1)
            pool.wait_ge(idx_copied, 1)
            for f in range(FIELDS):
                gather(f, idx)
            nc.gpsimd.memset(ident[:], 0.0).then_inc(ident_cleared, 1)
            pool.wait_ge(ident_cleared, 1)
            nc.gpsimd.affine_select(out=ident[:], in_=ident[:], compare_op=ALU.not_equal, fill=1.0, base=0,
                                    pattern=[[-1, P]], channel_multiplier=1).then_inc(ident_made, 1)
            pool.wait_ge(gathered, 16 * FIELDS)
            nc.gpsimd.tensor_copy(idx[:], ids_all[:, 1, :]).then_inc(idx_copied, 1)
            pool.wait_ge(idx_copied, 2)
            pool.wait_ge(fields_copied, 2)
            for f in range(FIRST_TABLES):
                gather(f, idx)

            def tile(t, first=False, last=False):
                for q in range(QUARTERS):
                    for d in range(QDIMS):
                        i = QDIMS * q + d
                        n = t * SLABS + i
                        into = lanes[:, q % 2, d, 0:GROUP * S2]
                        if i == GATHER_SLAB and not last:
                            pool.wait_ge(gathered, (t + 2) * (16 * FIELDS))
                            nc.gpsimd.tensor_copy(idx[:].unsqueeze(1), ids_all[:, bass.ds(t + 2, 1), :]).then_inc(idx_copied, 1)
                            pool.wait_ge(idx_copied, t + 3)
                            pool.wait_ge(fields_copied, (t + 2) * 2)
                        if not (first and q < 2):
                            pool.wait_ge(fold_step, t * (FOLDS * QUARTERS) + (FOLDS * (q - 2) + 2))
                        for a in range(1, NA):
                            pool.wait_ge(parts_scaled, n * NA + (a + 1))
                            if a > 1:
                                pool.wait_ge(pool_added, n * POOL_ADDS + (a - 1))
                            nc.gpsimd.tensor_tensor(
                                out=into, in0=scaled[:, d % 2, 0, :] if a == 1 else into,
                                in1=scaled[:, d % 2, a, :], op=ALU.add).then_inc(pool_added, 1)
                        if i < LAST_SLAB and not last:
                            for f in range(FIRST_TABLES + LAST_TABLES * i // LAST_SLAB,
                                           FIRST_TABLES + LAST_TABLES * (i + 1) // LAST_SLAB):
                                gather(f, idx)
                        if i >= GATHER_SLAB and not last:
                            j = i - GATHER_SLAB
                            for f in range(FIRST_TABLES * j // LATE_SLABS, FIRST_TABLES * (j + 1) // LATE_SLABS):
                                gather(f, idx)

            tile(0, first=True)
            with pool.Fori(1, TILES - 1) as t:
                tile(t)
            tile(TILES - 1, last=True)
            pool.wait_ge(gathered, TILES * 16 * FIELDS + 16 * FIRST_TABLES)

        @block.scalar
        def _(act):
            def keep_fields_t(t, q, nth=None):
                act.wait_ge(fields_turned, t * QUARTERS + (q + 1))
                if nth not in (0, 1):
                    act.wait_ge(pairs_made, t * (QUARTERS * CHUNKS) + CHUNKS * (q - 1))
                nc.scalar.activation(fields_t[:, q % 2, :], turned[0:XFIELDS, q % 2, :],
                                     ACT.Copy).then_inc(fields_t_kept, 1)

            def keep_x1(quarter, parity, nth=None):
                act.wait_ge(pairs_used, quarter * CHUNKS + CHUNKS)
                if nth != 0:
                    act.wait_ge(x1_low_kept, quarter)
                    act.wait_ge(p1_part_made, quarter)
                nc.scalar.activation(x1_full[:], x1_sum[:], ACT.Relu, bias=b1_sb[:, 0:1]).then_inc(x1_full_kept, 1)
                if nth not in (0, 1):
                    act.wait_ge(parts_made, quarter * (GROUPS * QDIMS) - GROUPS * QDIMS)
                nc.scalar.activation(x1_high[:, parity, :], x1_sum[:], ACT.Relu,
                                     bias=b1_sb[:, 0:1]).then_inc(x1_high_kept, 1)

            act.wait_ge(top_loaded, 16 * TOP_LOADS)
            for quarter in range(AHEAD):
                keep_fields_t(0, quarter, nth=quarter)
            keep_x1(0, 0, nth=0)

            def tile(t, first=False, last=False):
                act.wait_ge(fields_copied, t * 2 + 2)
                if not first:
                    act.wait_ge(parts_scaled, t * (NA * SLABS))
                nc.scalar.activation(act_fields[:],
                                     fields[:, 0:2 * GROUP * NA, :].rearrange("p (g w) d -> p g (w d)", g=NA)
                                     [:, :, 0:GROUP * DIM], ACT.Copy).then_inc(act_fields_copied, 1)
                act.wait_ge(act_fields_copied, t + 1)
                for q in range(QUARTERS):
                    more = not (last and q == QUARTERS - 1)
                    for d in range(QDIMS):
                        i = QDIMS * q + d
                        n = t * SLABS + i
                        if not (first and i < 2):
                            act.wait_ge(pool_added, n * POOL_ADDS - POOL_ADDS)
                        for a, g in enumerate(A_GROUPS):
                            act.wait_ge(parts_made, n * GROUPS + (g + 1))
                            for j in range(GROUP):
                                at = DIM * j + i
                                last_one = nc.scalar.activation(
                                    scaled[:, d % 2, a, S2 * j:S2 * (j + 1)],
                                    parts[:, g % BANKS, S2 * j:S2 * (j + 1)], ACT.Copy,
                                    scale=act_fields[:, a, at:at + 1])
                            last_one.then_inc(parts_scaled, 1)
                            if (d, g) == X1_AT and more:
                                keep_x1(t * QUARTERS + (q + 1), (q + 1) % 2, nth=1 if first and q == 0 else None)
                            if (d, g) == KEEP_AT and not (last and q + AHEAD >= QUARTERS):
                                keep_fields_t(t + (q + AHEAD) // QUARTERS, (q + AHEAD) % QUARTERS)

            tile(0, first=True)
            with act.Fori(1, TILES - 1) as t:
                tile(t)
            tile(TILES - 1, last=True)

            def keep_p2(b):
                act.wait_ge(p2_turned, b + 1)
                nc.scalar.activation(p2_t[:, QCOLS * b:QCOLS * (b + 1)], turned[:, b % 2, :],
                                     ACT.Copy).then_inc(p2_kept, 1)

            def keep_h1(b):
                if b >= 2:
                    act.wait_ge(h2_made, C2 * (b - 1))
                for c in range(C1):
                    act.wait_ge(h1_made, C1 * b + c + 1)
                    nc.scalar.activation(h1_sb[:, b % 2, c, :], parts[:, c, :], ACT.Relu,
                                         bias=bt1_sb[:, c:c + 1]).then_inc(h1_kept, 1)

            def keep_h2(b):
                if b >= 2:
                    act.wait_ge(y_made, b - 1)
                for c in range(C2):
                    act.wait_ge(h2_made, C2 * b + c + 1)
                    bank = parts[:, 4, :] if c == 0 else x1_sum[:]
                    nc.scalar.activation(h2_sb[:, b % 2, c, :], bank, ACT.Relu,
                                         bias=bt2_sb[:, c:c + 1]).then_inc(h2_kept, 1)

            def keep_y(b):
                act.wait_ge(y_made, b + 1)
                nc.scalar.activation(y_row[:, QCOLS * b:QCOLS * (b + 1)], turned[0:1, b % 2, :],
                                     ACT.Copy).then_inc(y_kept, 1)

            act.wait_ge(pairs_made, TILES * QUARTERS * CHUNKS)
            for b in range(BLOCKS - 1):
                keep_p2(b)
            for step in range(BLOCKS + 2):
                if step < BLOCKS:
                    keep_h1(step)
                if step == 1:
                    act.wait_ge(pool_added, TILES * SLABS * POOL_ADDS)
                if 0 <= step - 1 < BLOCKS:
                    keep_h2(step - 1)
                if step == 1:
                    keep_p2(BLOCKS - 1)
                    act.wait_ge(p2_made, TILES)
                if 0 <= step - 2 < BLOCKS:
                    keep_y(step - 2)

        @block.vector
        def _(dve):
            def copy_fields(t, first=False):
                dve.wait_ge(gathered, t * (16 * FIELDS) + 16 * FIELDS)
                if not first:
                    dve.wait_ge(fields_turned, t * QUARTERS)
                    dve.wait_ge(act_fields_copied, t)
                    dve.wait_ge(dve_fields_copied, t)
                nc.vector.tensor_copy(fields[:, 0:FIELDS, :], rows[:]).then_inc(fields_copied, 1)
                nc.vector.tensor_copy(fields[:, FIELDS:XFIELDS, :], rows[:, 0:XFIELDS - FIELDS, :]).then_inc(fields_copied, 1)

            def make_pairs(t, q, c, nth=None):
                turns = t * (QUARTERS // 2) + (q // 2 + 1)
                dve.wait_ge(one_spread[q % 2], turns * (16 * CHUNK_SHIFTS))
                dve.wait_ge(other_spread[q % 2][c], turns * (16 * len(chunk_shifts(c))))
                if nth != 0:
                    dve.wait_ge(pairs_used, t * (CHUNKS * QUARTERS) + (CHUNKS * (q - 1) + c + 1))
                k = chunk_size(c)
                nc.vector.tensor_tensor(out=pairs[0:k, c, :], in0=one[0:k, q % 2, :], in1=other[0:k, q % 2, c, :],
                                        op=ALU.mult).then_inc(pairs_made, 1)

            def split_x1(quarter, parity, part, nth=None):
                dve.wait_ge(x1_full_kept, quarter + 1)
                dve.wait_ge(x1_high_kept, quarter + 1)
                if nth not in (0, 1):
                    dve.wait_ge(parts_made, quarter * (GROUPS * QDIMS) - GROUPS * QDIMS)
                nc.vector.tensor_tensor(out=x1_low[:, parity, :], in0=x1_full[:],
                                        in1=x1_high[:, parity, :].bitcast(f32), op=ALU.subtract).then_inc(x1_low_kept, 1)
                nc.vector.tensor_reduce(out=p1_part[:, part, :], in_=x1_full[:].rearrange("p (d b) -> p b d", d=QDIMS),
                                        op=ALU.add, axis=AX.X).then_inc(p1_part_made, 1)

            def fold(step, t, q):
                base = t * (FOLDS * QUARTERS) + FOLDS * q
                if step < 2:
                    d0 = 2 * step
                    dve.wait_ge(pool_added, t * (POOL_ADDS * SLABS) + POOL_ADDS * (QDIMS * q + d0 + 2))
                    dve.wait_ge(terms_added, t * (D_TERMS * SLABS) + D_TERMS * (QDIMS * q + d0 + 2))
                    nc.vector.tensor_tensor(out=folded[:, d0:d0 + 2, :], in0=lanes[:, q % 2, d0:d0 + 2, 0:3 * S2],
                                            in1=lanes[:, q % 2, d0:d0 + 2, 3 * S2:6 * S2],
                                            op=ALU.add).then_inc(fold_step, 1)
                elif step < 4:
                    dve.wait_ge(fold_step, base + step)
                    nc.vector.tensor_tensor(out=folded[:, :, 0:S2], in0=folded[:, :, 0:S2],
                                            in1=folded[:, :, S2 * (step - 1):S2 * step],
                                            op=ALU.add).then_inc(fold_step, 1)
                else:
                    dve.wait_ge(fold_step, base + step)
                    if q == 0:
                        nc.vector.tensor_scalar(out=relu_sum[:], in0=folded[:, :, 0:S2], scalar1=0.0, scalar2=None,
                                                op0=ALU.max).then_inc(fold_step, 1)
                    else:
                        nc.vector.scalar_tensor_tensor(out=relu_sum[:], in0=folded[:, :, 0:S2], scalar=0.0,
                                                       in1=relu_sum[:], op0=ALU.max, op1=ALU.add).then_inc(fold_step, 1)

            def keep_p2(t):
                dve.wait_ge(fold_step, t * (FOLDS * QUARTERS) + FOLDS * QUARTERS)
                nc.vector.tensor_reduce(out=p2[:, bass.ds(t, 1), :].rearrange("p a s -> p (a s)"),
                                        in_=relu_sum[:].rearrange("p d s -> p s d"),
                                        op=ALU.add, axis=AX.X).then_inc(p2_made, 1)

            dve.wait_ge(w2_loaded, 16)
            nc.vector.tensor_copy(w2_high[:], w2_raw).then_inc(w2_high_made, 1)
            dve.wait_ge(w2_high_made, 1)
            nc.vector.tensor_tensor(out=w2_low[:], in0=w2_raw, in1=w2_high[:].bitcast(f32),
                                    op=ALU.subtract).then_inc(w2_low_made, 1)
            dve.wait_ge(w1_loaded, 32)
            nc.vector.tensor_tensor(out=w1[:], in0=w1[:], in1=w1_other, op=ALU.add).then_inc(w1_made, 1)

            copy_fields(0, first=True)
            for c in range(CHUNKS):
                make_pairs(0, 0, c, nth=0)
            dve.wait_ge(top_loaded, 16 * TOP_LOADS)
            split_x1(0, 0, 0, nth=0)

            def tile(t, first=False, last=False):
                if not first:
                    dve.wait_ge(terms_added, t * (D_TERMS * SLABS))
                nc.vector.tensor_copy(dve_fields[:], fields[:, 0:FIELDS, :]).then_inc(dve_fields_copied, 1)
                dve.wait_ge(dve_fields_copied, t + 1)
                for q in range(QUARTERS):
                    quarter = t * QUARTERS + q
                    for d in range(QDIMS):
                        i = QDIMS * q + d
                        n = t * SLABS + i
                        made = 0
                        for g in D_GROUPS:
                            dve.wait_ge(parts_made, n * GROUPS + (g + 1))
                            for j, m in enumerate(GROUP_OF[g]):
                                into = lanes[:, q % 2, d, S2 * (GROUP + made % 2):S2 * (GROUP + made % 2 + 1)]
                                part = parts[:, g % BANKS, S2 * j:S2 * (j + 1)]
                                scale = dve_fields[:, m, i:i + 1]
                                if made == 1:
                                    nc.vector.tensor_scalar(out=into, in0=part, scalar1=scale, scalar2=None,
                                                            op0=ALU.mult).then_inc(terms_added, 1)
                                else:
                                    if made:
                                        dve.wait_ge(terms_added, n * D_TERMS + (made - 1))
                                    nc.vector.scalar_tensor_tensor(
                                        out=into, in0=part, scalar=scale, in1=into if made else b2_rows[:],
                                        op0=ALU.mult, op1=ALU.add).then_inc(terms_added, 1)
                                made += 1
                            if (d, g) == SPLIT_AT and not (last and q == QUARTERS - 1):
                                split_x1(t * QUARTERS + (q + 1), (q + 1) % 2, (q + 1) % QUARTERS,
                                         nth=1 if first and q == 0 else None)
                            if (d, g) == P1_AT and q == QUARTERS - 1:
                                dve.wait_ge(p1_part_made, t * QUARTERS + QUARTERS)
                                nc.vector.tensor_reduce(out=p1_t[:, bass.ds(t * P, P)],
                                                        in_=p1_part[:].rearrange("p q b -> p b q"),
                                                        op=ALU.add, axis=AX.X).then_inc(p1_made, 1)
                            if (d, g) == FIELDS_AT and q == 1 and not last:
                                copy_fields(t + 1)
                            coming = chunk_at(PAIRS_AT, FIRST_PAIRS_AT, (d, g), first and q == 0)
                            if coming:
                                lead, c = coming
                                if not (last and q + lead >= QUARTERS):
                                    make_pairs(t + (q + lead) // QUARTERS, (q + lead) % QUARTERS, c)
                            if (d, g) in FOLD_AT and not (first and q == 0):
                                before = (t, q - 1) if q else (t - 1, QUARTERS - 1)
                                fold(FOLD_AT[d, g], *before)
                            if (d, g) == P2_AT and q == 0 and not first:
                                keep_p2(t - 1)

            tile(0, first=True)
            with dve.Fori(1, TILES - 1) as t:
                tile(t)
            tile(TILES - 1, last=True)
            for step in range(FOLDS):
                fold(step, TILES - 1, QUARTERS - 1)
            keep_p2(TILES - 1)

        @block.tensor
        def _(pe):
            def turn_fields(t, q, nth=None):
                if nth is None and q == 0:
                    pe.wait_ge(fields_copied, t * 2 + 2)
                if nth not in (0, 1):
                    pe.wait_ge(fields_t_kept, t * QUARTERS + (q - 1))
                for d in range(QDIMS):
                    last_one = nc.tensor.transpose(turned[0:XFIELDS, q % 2, P * d:P * (d + 1)],
                                                   fields[:, :, QDIMS * q + d], ident[:])
                last_one.then_inc(fields_turned, 1)

            def use_pairs(c, quarter, head=False):
                k = chunk_size(c)
                pe.wait_ge(pairs_made, quarter * CHUNKS + (c + 1))
                if c == 0 and not head:
                    pe.wait_ge(x1_high_kept, quarter)
                nc.tensor.matmul(x1_sum[:], w1[0:k, c, :], pairs[0:k, c, :],
                                 start=(c == 0), stop=(c == CHUNKS - 1)).then_inc(pairs_used, 1)

            pe.wait_ge(ident_made, 1)
            pe.wait_ge(w1_made, 1)
            pe.wait_ge(fields_copied, 2)
            for quarter in range(AHEAD):
                turn_fields(0, quarter, nth=quarter)
            for c in range(CHUNKS):
                use_pairs(c, 0, head=True)
            pe.wait_ge(w2_low_made, 1)

            def tile(t, first=False, last=False):
                for q in range(QUARTERS):
                    quarter = t * QUARTERS + q
                    pe.wait_ge(x1_high_kept, quarter + 1)
                    pe.wait_ge(x1_low_kept, quarter + 1)
                    for d in range(QDIMS):
                        i = QDIMS * q + d
                        n = t * SLABS + i
                        high = x1_high[:, q % 2, P * d:P * (d + 1)]
                        low = x1_low[:, q % 2, P * d:P * (d + 1)]
                        for g in range(GROUPS):
                            if not (first and i == 0 and g < BANKS):
                                was = g - BANKS if g >= BANKS else g - BANKS + GROUPS
                                slab = n if g >= BANKS else n - 1
                                if was % 2 == 0:
                                    pe.wait_ge(parts_scaled, slab * NA + (was // 2 + 1))
                                else:
                                    pe.wait_ge(terms_added, slab * D_TERMS + D_UPTO[was])
                            m = GROUP_OF[g]
                            w = slice(S2 * m[0], S2 * (m[-1] + 1))
                            into = parts[:, g % BANKS, 0:S2 * len(m)]
                            nc.tensor.matmul(into, high, w2_high[:, w], start=True, stop=False)
                            nc.tensor.matmul(into, high, w2_low[:, w], start=False, stop=False)
                            nc.tensor.matmul(into, low, w2_high[:, w], start=False, stop=True).then_inc(parts_made, 1)
                            coming = chunk_at(USE_AT, FIRST_USE_AT, (d, g), first and q == 0)
                            if coming:
                                lead, c = coming
                                if not (last and q + lead >= QUARTERS):
                                    use_pairs(c, t * QUARTERS + (q + lead))
                            if (d, g) == TURN_AT and not (last and q + AHEAD >= QUARTERS):
                                turn_fields(t + (q + AHEAD) // QUARTERS, (q + AHEAD) % QUARTERS)

            tile(0, first=True)
            with pe.Fori(1, TILES - 1) as t:
                tile(t)
            tile(TILES - 1, last=True)

            pe.wait_ge(top_loaded, 16 * TOP_LOADS)
            pe.wait_ge(p1_made, TILES)
            pe.wait_ge(terms_added, TILES * SLABS * D_TERMS)
            pe.wait_ge(parts_scaled, TILES * SLABS * NA)

            def turn_p2(b):
                pe.wait_ge(p2_made, QCOLS // P * (b + 1))
                if b >= 2:
                    pe.wait_ge(p2_kept, b - 1)
                for j in range(QCOLS // P):
                    last_one = nc.tensor.transpose(turned[:, b % 2, P * j:P * (j + 1)],
                                                   p2[:, QCOLS // P * b + j, :], ident[:])
                last_one.then_inc(p2_turned, 1)

            def make_h1(b):
                cols = slice(QCOLS * b, QCOLS * (b + 1))
                pe.wait_ge(p2_kept, b + 1)
                for c in range(C1):
                    if b:
                        pe.wait_ge(h1_kept, C1 * (b - 1) + c + 1)
                    o = slice(P * c, P * (c + 1))
                    nc.tensor.matmul(parts[:, c, :], wt1_sb[:, 0, o], p1_t[:, cols], start=True, stop=False)
                    nc.tensor.matmul(parts[:, c, :], wt1_sb[:, 1, o], p2_t[:, cols], start=False, stop=False)
                    nc.tensor.matmul(parts[:, c, :], wt1_dense[:, o], dense_sb[:, cols],
                                     start=False, stop=True).then_inc(h1_made, 1)

            def make_h2(b):
                for c in range(C2):
                    if b:
                        pe.wait_ge(h2_kept, C2 * (b - 1) + c + 1)
                    bank = parts[:, 4, :] if c == 0 else x1_sum[:]
                    for k in range(C1):
                        pe.wait_ge(h1_kept, C1 * b + k + 1)
                        last_one = nc.tensor.matmul(bank, wt2_sb[:, k, P * c:P * (c + 1)], h1_sb[:, b % 2, k, :],
                                                    start=(k == 0), stop=(k == C1 - 1))
                    last_one.then_inc(h2_made, 1)

            def make_y(b):
                pe.wait_ge(p2_kept, BLOCKS)
                if b >= 2:
                    pe.wait_ge(y_kept, b - 1)
                for k in range(C2):
                    pe.wait_ge(h2_kept, C2 * b + k + 1)
                    last_one = nc.tensor.matmul(turned[0:1, b % 2, :], wt3_sb[:, k:k + 1], h2_sb[:, b % 2, k, :],
                                                start=(k == 0), stop=(k == C2 - 1))
                last_one.then_inc(y_made, 1)

            for b in range(BLOCKS - 1):
                turn_p2(b)
            for step in range(BLOCKS + 2):
                if step < BLOCKS:
                    make_h1(step)
                if 0 <= step - 1 < BLOCKS:
                    make_h2(step - 1)
                if step == 1:
                    turn_p2(BLOCKS - 1)
                if 0 <= step - 2 < BLOCKS:
                    make_y(step - 2)


def kernel(**inputs):
    import numpy as np
    import concourse.bacc as bacc
    from concourse.bass_utils import run_bass_kernel_spmd

    nc = bacc.Bacc("TRN2", target_bir_lowering=False, num_devices=1)
    arrays = {}

    def given(name, a):
        a = np.ascontiguousarray(a)
        arrays[name] = a
        return nc.dram_tensor(name, a.shape, mybir.dt.from_np(a.dtype), kind="ExternalInput").ap()

    W1 = np.asarray(inputs["L0_rec_W1"])
    firsts, seconds = (list(x) for x in zip(*pair_rows()))
    w1_a = np.zeros((CHUNK * CHUNKS, S1), W1.dtype)
    w1_b = np.zeros((CHUNK * CHUNKS, S1), W1.dtype)
    w1_a[0:PAIRS] = W1[:, firsts, seconds].T
    w1_b[FIELDS:PAIRS] = W1[:, seconds[FIELDS:], firsts[FIELDS:]].T

    def by_chunk(w):
        return w.reshape(CHUNKS, CHUNK, S1).transpose(1, 0, 2)

    W2 = np.asarray(inputs["L0_rec_W2"])
    args = [
        given("dense_t", np.asarray(inputs["dense_ctx"]).T),
        given("ids", np.asarray(inputs["ids"])),
        [given(f"tbl_{f}", np.asarray(inputs[f"tbl_{f}"])) for f in range(FIELDS)],
        given("w1_a", by_chunk(w1_a)),
        given("w1_b", by_chunk(w1_b)),
        given("b1", np.asarray(inputs["L0_rec_b1"]).reshape(S1, 1)),
        given("w2_t", W2.transpose(1, 2, 0).reshape(S1, FIELDS * S2)),
        given("b2", np.asarray(inputs["L0_rec_b2"])),
        given("wt1", np.asarray(inputs["W_top1"])),
        given("bt1", np.asarray(inputs["b_top1"]).reshape(H1 // P, P).T),
        given("wt2", np.asarray(inputs["W_top2"])),
        given("bt2", np.asarray(inputs["b_top2"]).reshape(H2 // P, P).T),
        given("wt3", np.asarray(inputs["W_top3"]).reshape(H2 // P, P).T),
    ]
    out = nc.dram_tensor("y", (1, BATCH), mybir.dt.float32, kind="ExternalOutput").ap()
    dlrm_tower(nc, *args, out)
    r = run_bass_kernel_spmd(nc, [arrays], core_ids=[0])
    return r.results[0]["y"].reshape(BATCH, 1)
```

```python
import concourse.bass as bass
from concourse import mybir
from contextlib import ExitStack

BATCH = 2048
FIELDS = 39
DIM = 16
S1 = 128
S2 = 128
DENSE = 16
H1 = 512
H2 = 256

P = 128
TILES = BATCH // P
QUARTERS = 4
QDIMS = DIM // QUARTERS
QCOLS = QDIMS * P
SLABS = QUARTERS * QDIMS

SHIFTS = FIELDS // 2 + 1
CHUNK_SHIFTS = 3
CHUNKS = SHIFTS // CHUNK_SHIFTS
SHIFTED = CHUNK_SHIFTS * FIELDS
EXTRA = P - SHIFTED
K18, K19 = SHIFTS - 2, SHIFTS - 1
EXTRA_PARTNERS = sorted([K18, K19, FIELDS - K18, FIELDS - K19])
REST_RUNS = [(m, (m + k) % FIELDS, n)
             for k in (K18, K19)
             for m, n in ((EXTRA, FIELDS - k - EXTRA), (FIELDS - k + EXTRA, k - EXTRA))]
REST = sum(n for _, _, n in REST_RUNS)
REST_ROWS = 3 * REST
XFIELDS = 66

GROUP = 4
GROUPS = -(-FIELDS // GROUP)
GROUP_OF = [list(range(GROUP * g, min(GROUP * g + GROUP, FIELDS))) for g in range(GROUPS)]
BANKS = 5
A_GROUPS = list(range(0, GROUPS, 2))
D_GROUPS = list(range(1, GROUPS, 2))
NA = len(A_GROUPS)
D_TERMS = sum(len(GROUP_OF[g]) for g in D_GROUPS)
D_UPTO = {g: sum(len(GROUP_OF[x]) for x in D_GROUPS if x <= g) for g in D_GROUPS}
POOL_ADDS = 3
LANES = GROUP + 2
FOLDS = 5

FIELDS_AT = (2, 4)
TURN_AT = (2, 9)
KEEP_AT = (3, 0)
PAIRS_AT = {(2, 5): (2, 0), (2, 9): (2, 1), (3, 1): (2, 2), (3, 3): (2, 3),
            (0, 1): (1, 4), (0, 3): (1, 5)}
USE_AT = {(3, 0): (2, 0), (3, 3): (2, 1), (3, 6): (2, 2), (3, 9): (2, 3),
          (0, 5): (1, 4), (0, 9): (1, 5), (1, 2): (1, CHUNKS)}
REST_AT = {(0, 9): (2, 0)}
REST_HIGH_AT = {(2, 2): (2, 0)}
REST_LOW_AT = {(2, 7): (2, 0)}
FIRST_PAIRS_AT = {(0, 1): (1, 0), (0, 3): (1, 1), (0, 5): (1, 2), (0, 7): (1, 3),
                  (0, 9): (1, 4), (1, 3): (1, 5)}
FIRST_USE_AT = {(0, 5): (1, 0), (0, 7): (1, 1), (0, 9): (1, 2), (1, 1): (1, 3),
                (1, 3): (1, 4), (1, 6): (1, 5), (2, 1): (1, CHUNKS)}
FIRST_REST_AT = {(0, 7): (1, 0), (2, 7): (2, 0)}
FIRST_REST_HIGH_AT = {(0, 8): (1, 0), (3, 0): (2, 0)}
FIRST_REST_LOW_AT = {(1, 1): (1, 0), (3, 7): (2, 0)}
FIRST_X1_AT = (2, 2)
X1_AT = (1, 4)
SPLIT_AT = (3, 5)
FOLD_AT = {(0, 5): 0, (1, 1): 1, (1, 3): 2, (1, 7): 3, (2, 1): 4}
P1_AT = (2, 7)
P2_AT = (3, 9)
AHEAD = 3
TOP_PIECES = {"wt1": 2, "wt1_dense": 1, "p1": 3, "dense": 4, "wt2": 2, "last_p1": 1}
TOP_HIGH_AT = {(2, 2, 2): ("wt1", 0), (2, 2, 4): ("wt1", 1), (2, 2, 6): ("wt1_dense", 0), (2, 2, 8): ("p1", 0),
               (2, 3, 0): ("p1", 1), (2, 3, 2): ("p1", 2), (3, 0, 4): ("dense", 0), (3, 0, 6): ("dense", 1),
               (3, 0, 8): ("dense", 2), (3, 1, 0): ("dense", 3)}
TOP_LOW_AT = {(2, 2, 5): ("wt1", 0), (2, 2, 7): ("wt1", 1), (2, 2, 9): ("wt1_dense", 0), (2, 3, 1): ("p1", 0),
              (2, 3, 3): ("p1", 1), (3, 0, 1): ("p1", 2), (3, 0, 9): ("dense", 0), (3, 2, 5): ("dense", 1),
              (3, 3, 1): ("dense", 2), (3, 3, 3): ("dense", 3)}

GATHER_SLAB = 6
FIRST_TABLES = 26
LAST_SLAB = 5
LAST_TABLES = FIELDS - FIRST_TABLES
LATE_SLABS = SLABS - GATHER_SLAB


def chunk_at(places, first_places, here, first_quarter):
    if not first_quarter:
        return places.get(here)
    if 2 in (what[0] for what in first_places.values()):
        return first_places.get(here)
    two_ahead = {at: what for at, what in places.items() if what[0] == 2}
    return {**two_ahead, **first_places}.get(here)


def chunk_runs(c):
    runs = [(FIELDS * i, 0, CHUNK_SHIFTS * c + i, FIELDS) for i in range(CHUNK_SHIFTS)]
    if c < len(EXTRA_PARTNERS):
        runs.append((SHIFTED, 0, EXTRA_PARTNERS[c], EXTRA))
    return runs


def chunk_size(c):
    return sum(n for _, _, _, n in chunk_runs(c))


def dlrm_tower(nc, dense_t, ids, tables, w1_a, w1_b, w1_rest_a, w1_rest_b, b1, w2_t, b2, wt1, bt1, wt2, bt2, wt3, spread_from, out):
    f32 = mybir.dt.float32
    f32r = mybir.dt.float32r
    i32 = mybir.dt.int32
    ALU = mybir.AluOpType
    ACT = mybir.ActivationFunctionType
    AX = mybir.AxisListType

    C1, C2 = H1 // P, H2 // P
    BLOCKS = BATCH // QCOLS

    ctx = ExitStack()
    with ctx:
        def sb(name, shape, dt=f32):
            return ctx.enter_context(nc.sbuf_tensor(name, shape, dt))

        def sem(name):
            return ctx.enter_context(nc.semaphore(name))

        ids_all = sb("ids_all", [P, TILES + 1, FIELDS], i32)
        idx = sb("idx", [P, FIELDS], i32)
        rows = sb("rows", [P, FIELDS, DIM])
        fields = sb("fields", [P, XFIELDS, DIM])
        act_fields = sb("act_fields", [P, NA, GROUP * DIM])
        dve_fields = sb("dve_fields", [P, FIELDS, DIM])
        fields_t = sb("fields_t", [XFIELDS, 2, QCOLS])
        one = sb("one", [P, 2, QCOLS], f32r)[:].bitcast(f32)
        other = sb("other", [P, 2, CHUNKS, QCOLS], f32r)[:].bitcast(f32)
        rest_one = sb("rest_one", [REST, 2, QCOLS])
        rest_other = sb("rest_other", [REST, 2, QCOLS])
        pairs = sb("pairs", [P, CHUNKS, QCOLS])
        rest_pairs = sb("rest_pairs", [REST, QCOLS])
        rest = sb("rest", [REST_ROWS, QCOLS], f32r)
        rest_low = sb("rest_low", [REST, QCOLS], f32r)
        w1 = sb("w1", [P, CHUNKS, S1])
        w1_rest = sb("w1_rest", [REST_ROWS, S1], f32r)
        w2_high = sb("w2_high", [P, FIELDS * S2], f32r)
        w2_low = sb("w2_low", [P, FIELDS * S2], f32r)
        x1_full = sb("x1_full", [P, QCOLS])
        x1_high = sb("x1_high", [P, 2, QCOLS], f32r)
        x1_low = sb("x1_low", [P, 2, QCOLS], f32r)
        scaled = sb("scaled", [P, 2, NA, GROUP * S2])
        lanes = sb("lanes", [P, 2, QDIMS, LANES * S2])
        folded = sb("folded", [P, QDIMS, 3 * S2])
        relu_sum = sb("relu_sum", [P, QDIMS, S2])
        p1_part = sb("p1_part", [P, QUARTERS, P])
        p1_t = sb("p1_t", [P, BATCH])
        p2 = sb("p2", [P, TILES, S2])
        wt1_sb = sb("wt1_sb", [P, 2, H1])
        wt1_dense = sb("wt1_dense", [DENSE, H1])
        wt2_sb = sb("wt2_sb", [P, H1 // P, H2])
        wt3_sb = sb("wt3_sb", [P, H2 // P])
        b1_sb = sb("b1_sb", [P, 1])
        b2_rows = sb("b2_rows", [P, S2])
        bt1_sb = sb("bt1_sb", [P, H1 // P])
        bt2_sb = sb("bt2_sb", [P, H2 // P])
        ident = sb("ident", [P, P])

        rest_bits = rest[:].bitcast(f32)
        rest_low_bits = rest_low[:].bitcast(f32)
        w1_rest_bits = w1_rest[:].bitcast(f32)

        w2_raw = lanes[:].rearrange("p a d n -> p (a d n)")[:, 0:FIELDS * S2]
        after = scaled[:].rearrange("p a g n -> p (a g n)")
        w1_other = after[:, 0:CHUNKS * S1].rearrange("p (c s) -> p c s", s=S1)
        w1_rest_a_sb = after[0:REST, CHUNKS * S1:(CHUNKS + 1) * S1]
        w1_rest_b_sb = after[0:REST, (CHUNKS + 1) * S1:(CHUNKS + 2) * S1]
        top_parts = other.rearrange("p a c n -> p (a c n)").bitcast(f32r)
        before_last = BATCH - QCOLS
        last_p1_parts = x1_low[:]
        p1_high = top_parts[:, 0:before_last]
        p1_low = top_parts[:, before_last:2 * before_last]
        dense_parts = top_parts[0:3 * DENSE, 2 * before_last:2 * before_last + BATCH]
        wt1_dense_parts = rest[0:3 * DENSE, :]
        wt1_whole = wt1_sb[:].rearrange("p c n -> p (c n)")
        wt1_high = one.rearrange("p a n -> p (a n)").bitcast(f32r)
        wt1_low = top_parts[:, 2 * before_last + BATCH:2 * before_last + BATCH + 2 * H1]
        wt2_whole = wt2_sb[:].rearrange("p c n -> p (c n)")
        wt2_high = x1_high[:].rearrange("p a n -> p (a n)")
        wt2_low = [w[:, 2 * BATCH:2 * BATCH + QCOLS] for w in (w2_high, w2_low)]
        dense_sb = pairs[:].rearrange("p c n -> p (c n)")[0:DENSE, 0:BATCH]
        h1_full = [pairs[:, BLOCKS, :], pairs[:, BLOCKS + 1, :], x1_full[:], p1_part[:].rearrange("p q b -> p (q b)")]
        p2_high = w2_high[:, 0:BATCH]
        p2_low = w2_low[:, 0:BATCH]
        h1_high = w2_high[:, BATCH:BATCH + C1 * QCOLS].rearrange("p (c n) -> p c n", n=QCOLS)
        h1_low = w2_low[:, BATCH:BATCH + C1 * QCOLS].rearrange("p (c n) -> p c n", n=QCOLS)
        h2_sb = after[:, 0:2 * C2 * QCOLS].rearrange("p (a c n) -> p a c n", a=2, n=QCOLS)
        y_row = lanes[:].rearrange("p a d n -> p (a d n)")[0:1, 0:BATCH]

        parts = ctx.enter_context(nc.psum_tensor("parts", [P, BANKS, 512], f32))
        turned = ctx.enter_context(nc.psum_tensor("turned", [P, 2, 512], f32))
        x1_sum = ctx.enter_context(nc.psum_tensor("x1_sum", [P, 512], f32))

        first_ids_loaded = sem("first_ids_loaded")
        ids_loaded = sem("ids_loaded")
        w1_loaded = sem("w1_loaded")
        w2_loaded = sem("w2_loaded")
        top_loaded = sem("top_loaded")
        ident_cleared = sem("ident_cleared")
        ident_made = sem("ident_made")
        w1_made = sem("w1_made")
        w2_high_made = sem("w2_high_made")
        w2_low_made = sem("w2_low_made")
        w1_rest_summed = sem("w1_rest_summed")
        w1_rest_high_made = sem("w1_rest_high_made")
        w1_rest_low_made = sem("w1_rest_low_made")
        w1_rest_copied = sem("w1_rest_copied")
        idx_copied = sem("idx_copied")
        gathered = sem("gathered")
        fields_copied = sem("fields_copied")
        act_fields_copied = sem("act_fields_copied")
        dve_fields_copied = sem("dve_fields_copied")
        fields_turned = sem("fields_turned")
        fields_t_kept = sem("fields_t_kept")
        fields_out = [sem(f"fields_out_{p}") for p in range(2)]
        one_spread = [sem(f"one_spread_{p}") for p in range(2)]
        other_spread = [[sem(f"other_spread_{p}_{c}") for c in range(CHUNKS)] for p in range(2)]
        rest_spread = [sem(f"rest_spread_{p}") for p in range(2)]
        pairs_made = sem("pairs_made")
        rest_made = sem("rest_made")
        rest_high_made = sem("rest_high_made")
        rest_low_made = sem("rest_low_made")
        rest_copied = sem("rest_copied")
        pairs_used = sem("pairs_used")
        x1_full_kept = sem("x1_full_kept")
        x1_high_kept = sem("x1_high_kept")
        x1_low_kept = sem("x1_low_kept")
        p1_part_made = sem("p1_part_made")
        p1_made = sem("p1_made")
        parts_made = sem("parts_made")
        parts_scaled = sem("parts_scaled")
        terms_added = sem("terms_added")
        pool_added = sem("pool_added")
        fold_step = sem("fold_step")
        p2_made = sem("p2_made")
        p2_turned = sem("p2_turned")
        top_high_made = {name: sem(f"{name}_high_made") for name in TOP_PIECES}
        top_low_made = {name: sem(f"{name}_low_made") for name in TOP_PIECES}
        dense_loaded = sem("dense_loaded")
        dense_copied = sem("dense_copied")
        p2_high_kept = sem("p2_high_kept")
        p2_low_kept = sem("p2_low_kept")
        h1_made = sem("h1_made")
        h1_used = sem("h1_used")
        h1_full_kept = sem("h1_full_kept")
        h1_high_kept = sem("h1_high_kept")
        h1_low_kept = sem("h1_low_kept")
        h2_kept = sem("h2_kept")
        y_made = sem("y_made")
        y_kept = sem("y_kept")
        stored = sem("stored")

        USES = CHUNKS + 1
        REST_COPIES = 16 * 2 * len(REST_RUNS)
        TOP_LOADS = 8

        block = ctx.enter_context(nc.Block())

        @block.sync
        def _(sp):
            sp.dma_start(ids_all[:, 0:1, :], ids[0:P, :].rearrange("(t p) f -> p t f", p=P)).then_inc(first_ids_loaded, 16)
            sp.dma_start(ids_all[:, 1:TILES, :],
                         ids[P:BATCH, :].rearrange("(t p) f -> p t f", p=P)).then_inc(ids_loaded, 16)
            sp.dma_start(ids_all[:, TILES:TILES + 1, :],
                         ids[0:P, :].rearrange("(t p) f -> p t f", p=P)).then_inc(ids_loaded, 16)
            sp.dma_start(w2_raw, w2_t).then_inc(w2_loaded, 16)
            sp.dma_start(b2_rows[:], bass.AP(tensor=b2.tensor, offset=b2.offset,
                                             ap=[[0, P], [1, S2]])).then_inc(top_loaded, 16)
            sp.dma_start(w1[:], w1_a).then_inc(w1_loaded, 16)
            sp.dma_start(w1_other, w1_b).then_inc(w1_loaded, 16)
            sp.dma_start(w1_rest_a_sb, w1_rest_a).then_inc(w1_loaded, 16)
            sp.dma_start(w1_rest_b_sb, w1_rest_b).then_inc(w1_loaded, 16)
            sp.dma_start(b1_sb[:], b1).then_inc(top_loaded, 16)
            sp.dma_start(wt1_sb[:], wt1[0:2 * P, :].rearrange("(c p) n -> p c n", p=P)).then_inc(top_loaded, 16)
            sp.dma_start(wt1_dense[:], wt1[2 * P:2 * P + DENSE, :]).then_inc(top_loaded, 16)
            sp.dma_start(wt2_sb[:], wt2.rearrange("(c p) n -> p c n", p=P)).then_inc(top_loaded, 16)
            sp.dma_start(wt3_sb[:], wt3).then_inc(top_loaded, 16)
            sp.dma_start(bt1_sb[:], bt1).then_inc(top_loaded, 16)
            sp.dma_start(bt2_sb[:], bt2).then_inc(top_loaded, 16)

            def spread_rest(p):
                row = 0
                for m, partner, n in REST_RUNS:
                    sp.dma_start(rest_one[row:row + n, p, :], fields_t[m:m + n, p, :]).then_inc(rest_spread[p], 16)
                    sp.dma_start(rest_other[row:row + n, p, :],
                                 fields_t[partner:partner + n, p, :]).then_inc(rest_spread[p], 16)
                    row += n

            def from_dram(p, first, *steps):
                row = spread_from[p, first:first + 1, :]
                return bass.AP(tensor=row.tensor, offset=row.offset, ap=[*steps, [1, QCOLS]])

            def spread_fields(t, q):
                sp.wait_ge(fields_t_kept, t * QUARTERS + (q + 1))
                p = q % 2
                sp.dma_start(spread_from[p], fields_t[:, p, :]).then_inc(fields_out[p], 16)
                spread_rest(p)
                sp.wait_ge(fields_out[p], t * (16 * QUARTERS // 2) + 16 * (q // 2 + 1))
                sp.dma_start(one[0:SHIFTED, p, :], from_dram(p, 0, [0, CHUNK_SHIFTS], [QCOLS, FIELDS])).then_inc(one_spread[p], 16)
                sp.dma_start(one[SHIFTED:P, p, :], from_dram(p, 0, [QCOLS, EXTRA])).then_inc(one_spread[p], 16)
                sp.dma_start(other[SHIFTED:P, p, 0:len(EXTRA_PARTNERS), :],
                             from_dram(p, EXTRA_PARTNERS[0], [QCOLS, EXTRA], [QCOLS, len(EXTRA_PARTNERS)])
                             ).then_inc(one_spread[p], 16)
                for c in range(CHUNKS):
                    sp.dma_start(other[0:SHIFTED, p, c, :],
                                 from_dram(p, CHUNK_SHIFTS * c, [QCOLS, CHUNK_SHIFTS], [QCOLS, FIELDS])
                                 ).then_inc(other_spread[p][c], 16)

            def copy_rest(quarter):
                sp.wait_ge(rest_low_made, quarter + 1)
                sp.dma_start(rest_bits[REST:2 * REST, :], rest_bits[0:REST, :]).then_inc(rest_copied, 16)
                sp.dma_start(rest_bits[2 * REST:REST_ROWS, :], rest_low_bits).then_inc(rest_copied, 16)

            sp.wait_ge(w1_rest_low_made, 1)
            sp.dma_start(w1_rest_bits[REST:2 * REST, :], rest_low_bits[:, 0:S1]).then_inc(w1_rest_copied, 16)
            sp.dma_start(w1_rest_bits[2 * REST:REST_ROWS, :], w1_rest_bits[0:REST, :]).then_inc(w1_rest_copied, 16)

            for quarter in range(AHEAD):
                if quarter == 2:
                    copy_rest(1)
                spread_fields(0, quarter)

            def tile(t, last=False):
                for q in range(QUARTERS):
                    if not (last and q + 2 >= QUARTERS):
                        copy_rest(t * QUARTERS + (q + 2))
                    if not (last and q + AHEAD >= QUARTERS):
                        spread_fields(t + (q + AHEAD) // QUARTERS, (q + AHEAD) % QUARTERS)

            with sp.Fori(0, TILES - 1) as t:
                tile(t)
            tile(TILES - 1, last=True)
            sp.wait_ge(pairs_used, TILES * QUARTERS * USES)
            sp.dma_start(dense_sb, dense_t).then_inc(dense_loaded, 16)
            sp.wait_ge(top_low_made["wt1_dense"], 1)
            sp.dma_start(rest_bits[DENSE:2 * DENSE, :], wt1_dense[:]).then_inc(dense_copied, 16)
            sp.dma_start(rest_bits[2 * DENSE:3 * DENSE, :], rest_bits[0:DENSE, :]).then_inc(dense_copied, 16)
            sp.wait_ge(top_low_made["dense"], TOP_PIECES["dense"])
            dense_bits = dense_parts.bitcast(f32)
            sp.dma_start(dense_bits[DENSE:2 * DENSE, :], dense_bits[0:DENSE, :]).then_inc(dense_copied, 16)
            sp.dma_start(dense_bits[2 * DENSE:3 * DENSE, :], dense_sb).then_inc(dense_copied, 16)
            sp.wait_ge(y_kept, BLOCKS)
            sp.dma_start(out, y_row).then_inc(stored, 16)
            sp.wait_ge(stored, 16)

        @block.gpsimd
        def _(pool):
            def gather(f, rows_of):
                nc.gpsimd.indirect_dma_start(
                    out=rows[:, f, :], out_offset=None, in_=tables[f],
                    in_offset=bass.IndirectOffsetOnAxis(ap=rows_of[:, f:f + 1], axis=0),
                ).then_inc(gathered, 16)

            pool.wait_ge(first_ids_loaded, 16)
            nc.gpsimd.tensor_copy(idx[:], ids_all[:, 0, :]).then_inc(idx_copied, 1)
            pool.wait_ge(idx_copied, 1)
            for f in range(FIELDS):
                gather(f, idx)
            nc.gpsimd.memset(ident[:], 0.0).then_inc(ident_cleared, 1)
            pool.wait_ge(ident_cleared, 1)
            nc.gpsimd.affine_select(out=ident[:], in_=ident[:], compare_op=ALU.not_equal, fill=1.0, base=0,
                                    pattern=[[-1, P]], channel_multiplier=1).then_inc(ident_made, 1)
            pool.wait_ge(ids_loaded, 2 * 16)
            pool.wait_ge(gathered, 16 * FIELDS)
            nc.gpsimd.tensor_copy(idx[:], ids_all[:, 1, :]).then_inc(idx_copied, 1)
            pool.wait_ge(idx_copied, 2)
            pool.wait_ge(fields_copied, 2)
            for f in range(FIRST_TABLES):
                gather(f, idx)

            def tile(t, first=False, last=False):
                for q in range(QUARTERS):
                    for d in range(QDIMS):
                        i = QDIMS * q + d
                        n = t * SLABS + i
                        into = lanes[:, q % 2, d, 0:GROUP * S2]
                        if i == GATHER_SLAB and not last:
                            pool.wait_ge(gathered, (t + 2) * (16 * FIELDS))
                            nc.gpsimd.tensor_copy(idx[:].unsqueeze(1), ids_all[:, bass.ds(t + 2, 1), :]).then_inc(idx_copied, 1)
                            pool.wait_ge(idx_copied, t + 3)
                            pool.wait_ge(fields_copied, (t + 2) * 2)
                        if not (first and q < 2):
                            pool.wait_ge(fold_step, t * (FOLDS * QUARTERS) + (FOLDS * (q - 2) + 2))
                        pool.wait_ge(parts_scaled, n * NA + 4)
                        nc.gpsimd.tensor_tensor(out=scaled[:, d % 2, 0:2, :], in0=scaled[:, d % 2, 0:2, :],
                                                in1=scaled[:, d % 2, 2:4, :], op=ALU.add).then_inc(pool_added, 1)
                        pool.wait_ge(pool_added, n * POOL_ADDS + 1)
                        nc.gpsimd.tensor_tensor(out=into, in0=scaled[:, d % 2, 0, :],
                                                in1=scaled[:, d % 2, 1, :], op=ALU.add).then_inc(pool_added, 1)
                        pool.wait_ge(parts_scaled, n * NA + 5)
                        pool.wait_ge(pool_added, n * POOL_ADDS + 2)
                        nc.gpsimd.tensor_tensor(out=into, in0=into, in1=scaled[:, d % 2, 4, :],
                                                op=ALU.add).then_inc(pool_added, 1)
                        if i < LAST_SLAB and not last:
                            for f in range(FIRST_TABLES + LAST_TABLES * i // LAST_SLAB,
                                           FIRST_TABLES + LAST_TABLES * (i + 1) // LAST_SLAB):
                                gather(f, idx)
                        if i >= GATHER_SLAB and not last:
                            j = i - GATHER_SLAB
                            for f in range(FIRST_TABLES * j // LATE_SLABS, FIRST_TABLES * (j + 1) // LATE_SLABS):
                                gather(f, idx)

            tile(0, first=True)
            with pool.Fori(1, TILES - 1) as t:
                tile(t)
            tile(TILES - 1, last=True)
            pool.wait_ge(gathered, TILES * 16 * FIELDS + 16 * FIRST_TABLES)

        @block.scalar
        def _(act):
            def keep_fields_t(t, q, nth=None):
                act.wait_ge(fields_turned, t * QUARTERS + (q + 1))
                if nth not in (0, 1):
                    act.wait_ge(pairs_made, t * (QUARTERS * CHUNKS) + CHUNKS * (q - 1))
                    act.wait_ge(rest_made, t * QUARTERS + (q - 1))
                nc.scalar.activation(fields_t[:, q % 2, :], turned[0:XFIELDS, q % 2, :],
                                     ACT.Copy).then_inc(fields_t_kept, 1)

            def copy_fields(t):
                act.wait_ge(gathered, t * (16 * FIELDS) + 16 * FIELDS)
                act.wait_ge(fields_turned, t * QUARTERS)
                act.wait_ge(act_fields_copied, t)
                act.wait_ge(dve_fields_copied, t)
                nc.scalar.activation(fields[:, 0:FIELDS, :], rows[:], ACT.Copy).then_inc(fields_copied, 1)
                nc.scalar.activation(fields[:, FIELDS:XFIELDS, :], rows[:, 0:XFIELDS - FIELDS, :],
                                     ACT.Copy).then_inc(fields_copied, 1)

            def make_rest_high(quarter, nth=None):
                act.wait_ge(rest_made, quarter + 1)
                if nth != 0:
                    act.wait_ge(pairs_used, quarter * USES)
                nc.scalar.activation(rest[0:REST, :], rest_pairs[:], ACT.Copy).then_inc(rest_high_made, 1)

            def keep_x1(quarter, parity, nth=None):
                act.wait_ge(pairs_used, quarter * USES + USES)
                if nth != 0:
                    act.wait_ge(x1_low_kept, quarter)
                    act.wait_ge(p1_part_made, quarter)
                nc.scalar.activation(x1_full[:], x1_sum[:], ACT.Relu, bias=b1_sb[:, 0:1]).then_inc(x1_full_kept, 1)
                if nth not in (0, 1):
                    act.wait_ge(parts_made, quarter * (GROUPS * QDIMS) - GROUPS * QDIMS)
                nc.scalar.activation(x1_high[:, parity, :], x1_sum[:], ACT.Relu,
                                     bias=b1_sb[:, 0:1]).then_inc(x1_high_kept, 1)

            act.wait_ge(w1_rest_summed, 1)
            nc.scalar.activation(w1_rest[0:REST, :], w1_rest_a_sb, ACT.Copy).then_inc(w1_rest_high_made, 1)
            act.wait_ge(top_loaded, 16 * TOP_LOADS)
            keep_fields_t(0, 0, nth=0)
            keep_fields_t(0, 1, nth=1)
            make_rest_high(0, nth=0)
            act.wait_ge(rest_low_made, 1)
            act.dma_start(rest_bits[REST:2 * REST, :], rest_bits[0:REST, :]).then_inc(rest_copied, 16)
            act.dma_start(rest_bits[2 * REST:REST_ROWS, :], rest_low_bits).then_inc(rest_copied, 16)
            keep_fields_t(0, 2)
            keep_x1(0, 0, nth=0)

            def make_top_high(name, piece):
                if (name, piece) == ("wt1", 0):
                    act.wait_ge(pairs_made, TILES * QUARTERS * CHUNKS)
                    act.wait_ge(pairs_used, TILES * QUARTERS * USES)
                if (name, piece) == ("dense", 0):
                    act.wait_ge(dense_loaded, 16)
                if name == "last_p1":
                    act.wait_ge(p1_made, TILES)
                if (name, piece) == ("p1", 0):
                    act.wait_ge(p1_made, TILES - QCOLS // P)
                into, whole = {
                    "wt1": (wt1_high, wt1_whole),
                    "wt1_dense": (wt1_dense_parts[0:DENSE, :], wt1_dense[:]),
                    "wt2": (wt2_high, wt2_whole),
                    "p1": (p1_high, p1_t[:, 0:before_last]),
                    "dense": (dense_parts[0:DENSE, :], dense_sb),
                    "last_p1": (last_p1_parts[:, 0, :], p1_t[:, before_last:BATCH]),
                }[name]
                cols = slice(QCOLS * piece, QCOLS * (piece + 1))
                nc.scalar.activation(into[:, cols], whole[:, cols], ACT.Copy).then_inc(top_high_made[name], 1)

            def tile(t, first=False, last=False):
                act.wait_ge(fields_copied, t * 2 + 2)
                if not first:
                    act.wait_ge(parts_scaled, t * (NA * SLABS))
                nc.scalar.activation(act_fields[:],
                                     fields[:, 0:2 * GROUP * NA, :].rearrange("p (g w) d -> p g (w d)", g=NA)
                                     [:, :, 0:GROUP * DIM], ACT.Copy).then_inc(act_fields_copied, 1)
                act.wait_ge(act_fields_copied, t + 1)
                for q in range(QUARTERS):
                    more = not (last and q == QUARTERS - 1)
                    for d in range(QDIMS):
                        i = QDIMS * q + d
                        n = t * SLABS + i
                        if not (first and i < 2):
                            act.wait_ge(pool_added, n * POOL_ADDS - POOL_ADDS)
                        for a, g in enumerate(A_GROUPS):
                            act.wait_ge(parts_made, n * GROUPS + (g + 1))
                            for j in range(GROUP):
                                at = DIM * j + i
                                last_one = nc.scalar.activation(
                                    scaled[:, d % 2, a, S2 * j:S2 * (j + 1)],
                                    parts[:, g % BANKS, S2 * j:S2 * (j + 1)], ACT.Copy,
                                    scale=act_fields[:, a, at:at + 1])
                            last_one.then_inc(parts_scaled, 1)
                            if last and (q, d, g) in TOP_HIGH_AT:
                                make_top_high(*TOP_HIGH_AT[q, d, g])
                            coming = chunk_at(REST_HIGH_AT, FIRST_REST_HIGH_AT, (d, g), first and q == 0)
                            if coming and not (last and q + coming[0] >= QUARTERS):
                                make_rest_high(t * QUARTERS + (q + coming[0]))
                            if (d, g) == (FIRST_X1_AT if first and q == 0 else X1_AT) and more:
                                keep_x1(t * QUARTERS + (q + 1), (q + 1) % 2, nth=1 if first and q == 0 else None)
                            if (d, g) == FIELDS_AT and q == 1 and not last:
                                copy_fields(t + 1)
                            if (d, g) == KEEP_AT and not (last and q + AHEAD >= QUARTERS):
                                keep_fields_t(t + (q + AHEAD) // QUARTERS, (q + AHEAD) % QUARTERS)

            tile(0, first=True)
            with act.Fori(1, TILES - 1) as t:
                tile(t)
            tile(TILES - 1, last=True)

            def keep_p2_high(b):
                act.wait_ge(p2_turned, b + 1)
                nc.scalar.activation(p2_high[:, QCOLS * b:QCOLS * (b + 1)], turned[:, b % 2, :],
                                     ACT.Copy).then_inc(p2_high_kept, 1)

            def keep_h1(b):
                for c in range(C1):
                    i = C1 * b + c
                    act.wait_ge(h1_made, i + 1)
                    if b:
                        act.wait_ge(h1_low_kept, i - C1 + 1)
                    nc.scalar.activation(h1_full[c], parts[:, c, :], ACT.Relu,
                                         bias=bt1_sb[:, c:c + 1]).then_inc(h1_full_kept, 1)
                    if b:
                        act.wait_ge(h1_used, i - C1 + 1)
                    nc.scalar.activation(h1_high[:, c, :], parts[:, c, :], ACT.Relu,
                                         bias=bt1_sb[:, c:c + 1]).then_inc(h1_high_kept, 1)

            def keep_h2(b):
                if b >= 2:
                    act.wait_ge(y_made, b - 1)
                for c in range(C2):
                    act.wait_ge(h1_used, C1 * b + C1)
                    bank = parts[:, 4, :] if c == 0 else x1_sum[:]
                    nc.scalar.activation(h2_sb[:, b % 2, c, :], bank, ACT.Relu,
                                         bias=bt2_sb[:, c:c + 1]).then_inc(h2_kept, 1)

            def keep_y(b):
                act.wait_ge(y_made, b + 1)
                nc.scalar.activation(y_row[:, QCOLS * b:QCOLS * (b + 1)], turned[0:1, b % 2, :],
                                     ACT.Copy).then_inc(y_kept, 1)

            act.wait_ge(parts_made, TILES * SLABS * GROUPS)
            keep_p2_high(0)
            keep_p2_high(1)
            make_top_high("wt2", 0)
            make_top_high("wt2", 1)
            make_top_high("last_p1", 0)
            for step in range(BLOCKS + 2):
                if step < BLOCKS:
                    keep_h1(step)
                if step == 1:
                    act.wait_ge(pool_added, TILES * SLABS * POOL_ADDS)
                if step < 2:
                    keep_p2_high(step + 2)
                if 0 <= step - 1 < BLOCKS:
                    keep_h2(step - 1)
                if step == 1:
                    act.wait_ge(p2_made, TILES)
                if 0 <= step - 2 < BLOCKS:
                    keep_y(step - 2)

        @block.vector
        def _(dve):
            def make_pairs(t, q, c, nth=None):
                turns = t * (QUARTERS // 2) + (q // 2 + 1)
                dve.wait_ge(one_spread[q % 2], turns * (3 * 16))
                dve.wait_ge(other_spread[q % 2][c], turns * 16)
                if nth != 0:
                    dve.wait_ge(pairs_used, t * (USES * QUARTERS) + (USES * (q - 1) + c + 1))
                k = chunk_size(c)
                nc.vector.tensor_tensor(out=pairs[0:k, c, :], in0=one[0:k, q % 2, :], in1=other[0:k, q % 2, c, :],
                                        op=ALU.mult).then_inc(pairs_made, 1)

            def make_rest(t, q, nth=None):
                dve.wait_ge(rest_spread[q % 2], t * (REST_COPIES * QUARTERS // 2) + REST_COPIES * (q // 2 + 1))
                if nth != 0:
                    dve.wait_ge(rest_low_made, t * QUARTERS + q)
                nc.vector.tensor_tensor(out=rest_pairs[:], in0=rest_one[:, q % 2, :], in1=rest_other[:, q % 2, :],
                                        op=ALU.mult).then_inc(rest_made, 1)

            def make_rest_low(quarter, nth=None):
                dve.wait_ge(rest_high_made, quarter + 1)
                if nth == 0:
                    dve.wait_ge(w1_rest_copied, 32)
                else:
                    dve.wait_ge(rest_copied, quarter * 32)
                nc.vector.tensor_tensor(out=rest_low[:], in0=rest_pairs[:], in1=rest[0:REST, :].bitcast(f32),
                                        op=ALU.subtract).then_inc(rest_low_made, 1)

            def split_x1(quarter, parity, part, nth=None):
                dve.wait_ge(x1_full_kept, quarter + 1)
                dve.wait_ge(x1_high_kept, quarter + 1)
                if nth not in (0, 1):
                    dve.wait_ge(parts_made, quarter * (GROUPS * QDIMS) - GROUPS * QDIMS)
                nc.vector.tensor_tensor(out=x1_low[:, parity, :], in0=x1_full[:],
                                        in1=x1_high[:, parity, :].bitcast(f32), op=ALU.subtract).then_inc(x1_low_kept, 1)
                nc.vector.tensor_reduce(out=p1_part[:, part, :], in_=x1_full[:].rearrange("p (d b) -> p b d", d=QDIMS),
                                        op=ALU.add, axis=AX.X).then_inc(p1_part_made, 1)

            def fold(step, t, q):
                base = t * (FOLDS * QUARTERS) + FOLDS * q
                if step < 2:
                    d0 = 2 * step
                    dve.wait_ge(pool_added, t * (POOL_ADDS * SLABS) + POOL_ADDS * (QDIMS * q + d0 + 2))
                    dve.wait_ge(terms_added, t * (D_TERMS * SLABS) + D_TERMS * (QDIMS * q + d0 + 2))
                    nc.vector.tensor_tensor(out=folded[:, d0:d0 + 2, :], in0=lanes[:, q % 2, d0:d0 + 2, 0:3 * S2],
                                            in1=lanes[:, q % 2, d0:d0 + 2, 3 * S2:6 * S2],
                                            op=ALU.add).then_inc(fold_step, 1)
                elif step < 4:
                    dve.wait_ge(fold_step, base + step)
                    nc.vector.tensor_tensor(out=folded[:, :, 0:S2], in0=folded[:, :, 0:S2],
                                            in1=folded[:, :, S2 * (step - 1):S2 * step],
                                            op=ALU.add).then_inc(fold_step, 1)
                else:
                    dve.wait_ge(fold_step, base + step)
                    if q == 0:
                        nc.vector.tensor_scalar(out=relu_sum[:], in0=folded[:, :, 0:S2], scalar1=0.0, scalar2=None,
                                                op0=ALU.max).then_inc(fold_step, 1)
                    else:
                        nc.vector.scalar_tensor_tensor(out=relu_sum[:], in0=folded[:, :, 0:S2], scalar=0.0,
                                                       in1=relu_sum[:], op0=ALU.max, op1=ALU.add).then_inc(fold_step, 1)

            def keep_p2(t):
                dve.wait_ge(fold_step, t * (FOLDS * QUARTERS) + FOLDS * QUARTERS)
                nc.vector.tensor_reduce(out=p2[:, bass.ds(t, 1), :].rearrange("p a s -> p (a s)"),
                                        in_=relu_sum[:].rearrange("p d s -> p s d"),
                                        op=ALU.add, axis=AX.X).then_inc(p2_made, 1)

            def make_top_low(name, piece):
                dve.wait_ge(top_high_made[name], piece + 1)
                low, whole, high = {
                    "wt1": (wt1_low, wt1_whole, wt1_high),
                    "wt1_dense": (wt1_dense[:], wt1_dense[:], wt1_dense_parts[0:DENSE, :]),
                    "wt2": (wt2_low[piece % 2], wt2_whole, wt2_high),
                    "p1": (p1_low, p1_t[:, 0:before_last], p1_high),
                    "dense": (dense_sb, dense_sb, dense_parts[0:DENSE, :]),
                    "last_p1": (last_p1_parts[:, 1, :], p1_t[:, before_last:BATCH], last_p1_parts[:, 0, :]),
                }[name]
                cols = slice(QCOLS * piece, QCOLS * (piece + 1))
                nc.vector.tensor_tensor(out=low if name == "wt2" else low[:, cols], in0=whole[:, cols],
                                        in1=high[:, cols].bitcast(f32),
                                        op=ALU.subtract).then_inc(top_low_made[name], 1)

            def keep_p2_low(b):
                dve.wait_ge(p2_high_kept, b + 1)
                cols = slice(QCOLS * b, QCOLS * (b + 1))
                nc.vector.tensor_tensor(out=p2_low[:, cols], in0=turned[:, b % 2, :], in1=p2_high[:, cols].bitcast(f32),
                                        op=ALU.subtract).then_inc(p2_low_kept, 1)

            def keep_h1_low(b):
                for c in range(C1):
                    if b:
                        dve.wait_ge(h1_used, C1 * (b - 1) + c + 1)
                    dve.wait_ge(h1_full_kept, C1 * b + c + 1)
                    dve.wait_ge(h1_high_kept, C1 * b + c + 1)
                    nc.vector.tensor_tensor(out=h1_low[:, c, :], in0=h1_full[c],
                                            in1=h1_high[:, c, :].bitcast(f32),
                                            op=ALU.subtract).then_inc(h1_low_kept, 1)

            dve.wait_ge(w2_loaded, 16)
            nc.vector.tensor_copy(w2_high[:], w2_raw).then_inc(w2_high_made, 1)
            dve.wait_ge(w2_high_made, 1)
            nc.vector.tensor_tensor(out=w2_low[:], in0=w2_raw, in1=w2_high[:].bitcast(f32),
                                    op=ALU.subtract).then_inc(w2_low_made, 1)
            dve.wait_ge(w1_loaded, 4 * 16)
            nc.vector.tensor_tensor(out=w1[:], in0=w1[:], in1=w1_other, op=ALU.add).then_inc(w1_made, 1)
            nc.vector.tensor_tensor(out=w1_rest_a_sb, in0=w1_rest_a_sb, in1=w1_rest_b_sb,
                                    op=ALU.add).then_inc(w1_rest_summed, 1)
            dve.wait_ge(w1_rest_high_made, 1)
            nc.vector.tensor_tensor(out=rest_low[:, 0:S1], in0=w1_rest_a_sb, in1=w1_rest[0:REST, :].bitcast(f32),
                                    op=ALU.subtract).then_inc(w1_rest_low_made, 1)

            dve.wait_ge(gathered, 16 * FIELDS)
            nc.vector.tensor_copy(fields[:, 0:FIELDS, :], rows[:]).then_inc(fields_copied, 1)
            nc.vector.tensor_copy(fields[:, FIELDS:XFIELDS, :], rows[:, 0:XFIELDS - FIELDS, :]).then_inc(fields_copied, 1)
            make_rest(0, 0, nth=0)
            for c in range(CHUNKS):
                if c == 1:
                    make_rest_low(0, nth=0)
                make_pairs(0, 0, c, nth=0)
            dve.wait_ge(top_loaded, 16 * TOP_LOADS)
            split_x1(0, 0, 0, nth=0)

            def tile(t, first=False, last=False):
                if not first:
                    dve.wait_ge(terms_added, t * (D_TERMS * SLABS))
                nc.vector.tensor_copy(dve_fields[:], fields[:, 0:FIELDS, :]).then_inc(dve_fields_copied, 1)
                dve.wait_ge(dve_fields_copied, t + 1)
                for q in range(QUARTERS):
                    quarter = t * QUARTERS + q
                    for d in range(QDIMS):
                        i = QDIMS * q + d
                        n = t * SLABS + i
                        made = 0
                        for g in D_GROUPS:
                            dve.wait_ge(parts_made, n * GROUPS + (g + 1))
                            for j, m in enumerate(GROUP_OF[g]):
                                into = lanes[:, q % 2, d, S2 * (GROUP + made % 2):S2 * (GROUP + made % 2 + 1)]
                                part = parts[:, g % BANKS, S2 * j:S2 * (j + 1)]
                                scale = dve_fields[:, m, i:i + 1]
                                if made == 1:
                                    nc.vector.tensor_scalar(out=into, in0=part, scalar1=scale, scalar2=None,
                                                            op0=ALU.mult).then_inc(terms_added, 1)
                                else:
                                    if made:
                                        dve.wait_ge(terms_added, n * D_TERMS + (made - 1))
                                    nc.vector.scalar_tensor_tensor(
                                        out=into, in0=part, scalar=scale, in1=into if made else b2_rows[:],
                                        op0=ALU.mult, op1=ALU.add).then_inc(terms_added, 1)
                                made += 1
                            if (d, g) == SPLIT_AT and not (last and q == QUARTERS - 1):
                                split_x1(t * QUARTERS + (q + 1), (q + 1) % 2, (q + 1) % QUARTERS,
                                         nth=1 if first and q == 0 else None)
                            if (d, g) == P1_AT and q == QUARTERS - 1:
                                dve.wait_ge(p1_part_made, t * QUARTERS + QUARTERS)
                                nc.vector.tensor_reduce(out=p1_t[:, bass.ds(t * P, P)],
                                                        in_=p1_part[:].rearrange("p q b -> p b q"),
                                                        op=ALU.add, axis=AX.X).then_inc(p1_made, 1)
                            coming = chunk_at(REST_AT, FIRST_REST_AT, (d, g), first and q == 0)
                            if coming and not (last and q + coming[0] >= QUARTERS):
                                make_rest(t + (q + coming[0]) // QUARTERS, (q + coming[0]) % QUARTERS)
                            coming = chunk_at(REST_LOW_AT, FIRST_REST_LOW_AT, (d, g), first and q == 0)
                            if coming and not (last and q + coming[0] >= QUARTERS):
                                make_rest_low(t * QUARTERS + (q + coming[0]))
                            coming = chunk_at(PAIRS_AT, FIRST_PAIRS_AT, (d, g), first and q == 0)
                            if coming:
                                lead, c = coming
                                if not (last and q + lead >= QUARTERS):
                                    make_pairs(t + (q + lead) // QUARTERS, (q + lead) % QUARTERS, c)
                            if last and (q, d, g) in TOP_LOW_AT:
                                make_top_low(*TOP_LOW_AT[q, d, g])
                            if (d, g) in FOLD_AT and not (first and q == 0):
                                before = (t, q - 1) if q else (t - 1, QUARTERS - 1)
                                fold(FOLD_AT[d, g], *before)
                            if (d, g) == P2_AT and q == 0 and not first:
                                keep_p2(t - 1)

            tile(0, first=True)
            with dve.Fori(1, TILES - 1) as t:
                tile(t)
            tile(TILES - 1, last=True)
            keep_p2_low(0)
            keep_p2_low(1)
            for step in range(FOLDS):
                fold(step, TILES - 1, QUARTERS - 1)
            keep_p2(TILES - 1)
            make_top_low("wt2", 0)
            make_top_low("wt2", 1)
            make_top_low("last_p1", 0)
            for b in range(BLOCKS):
                keep_h1_low(b)
                if b < 2:
                    keep_p2_low(b + 2)

        @block.tensor
        def _(pe):
            def turn_fields(t, q, nth=None):
                if nth is None and q == 0:
                    pe.wait_ge(fields_copied, t * 2 + 2)
                if nth not in (0, 1):
                    pe.wait_ge(fields_t_kept, t * QUARTERS + (q - 1))
                for d in range(QDIMS):
                    last_one = nc.tensor.transpose(turned[0:XFIELDS, q % 2, P * d:P * (d + 1)],
                                                   fields[:, :, QDIMS * q + d], ident[:])
                last_one.then_inc(fields_turned, 1)

            def use_pairs(c, quarter, head=False):
                if c == CHUNKS:
                    pe.wait_ge(rest_copied, quarter * 32 + 32)
                    nc.tensor.matmul(x1_sum[:], w1_rest[:], rest[:], start=False, stop=True).then_inc(pairs_used, 1)
                    return
                k = chunk_size(c)
                pe.wait_ge(pairs_made, quarter * CHUNKS + (c + 1))
                if c == 0 and not head:
                    pe.wait_ge(x1_high_kept, quarter)
                nc.tensor.matmul(x1_sum[:], w1[0:k, c, :], pairs[0:k, c, :],
                                 start=(c == 0), stop=False).then_inc(pairs_used, 1)

            pe.wait_ge(ident_made, 1)
            pe.wait_ge(w1_made, 1)
            pe.wait_ge(fields_copied, 2)
            for quarter in range(AHEAD):
                turn_fields(0, quarter, nth=quarter)
            pe.wait_ge(w1_rest_copied, 32)
            for c in range(USES):
                use_pairs(c, 0, head=True)
            pe.wait_ge(w2_low_made, 1)

            def tile(t, first=False, last=False):
                for q in range(QUARTERS):
                    quarter = t * QUARTERS + q
                    pe.wait_ge(x1_high_kept, quarter + 1)
                    pe.wait_ge(x1_low_kept, quarter + 1)
                    for d in range(QDIMS):
                        i = QDIMS * q + d
                        n = t * SLABS + i
                        high = x1_high[:, q % 2, P * d:P * (d + 1)]
                        low = x1_low[:, q % 2, P * d:P * (d + 1)]
                        for g in range(GROUPS):
                            if not (first and i == 0 and g < BANKS):
                                was = g - BANKS if g >= BANKS else g - BANKS + GROUPS
                                slab = n if g >= BANKS else n - 1
                                if was % 2 == 0:
                                    pe.wait_ge(parts_scaled, slab * NA + (was // 2 + 1))
                                else:
                                    pe.wait_ge(terms_added, slab * D_TERMS + D_UPTO[was])
                            m = GROUP_OF[g]
                            w = slice(S2 * m[0], S2 * (m[-1] + 1))
                            into = parts[:, g % BANKS, 0:S2 * len(m)]
                            nc.tensor.matmul(into, high, w2_high[:, w], start=True, stop=False)
                            nc.tensor.matmul(into, high, w2_low[:, w], start=False, stop=False)
                            nc.tensor.matmul(into, low, w2_high[:, w], start=False, stop=True).then_inc(parts_made, 1)
                            coming = chunk_at(USE_AT, FIRST_USE_AT, (d, g), first and q == 0)
                            if coming:
                                lead, c = coming
                                if not (last and q + lead >= QUARTERS):
                                    use_pairs(c, t * QUARTERS + (q + lead))
                            if (d, g) == TURN_AT and not (last and q + AHEAD >= QUARTERS):
                                turn_fields(t + (q + AHEAD) // QUARTERS, (q + AHEAD) % QUARTERS)

            tile(0, first=True)
            with pe.Fori(1, TILES - 1) as t:
                tile(t)
            tile(TILES - 1, last=True)

            def turn_p2(b):
                pe.wait_ge(p2_made, QCOLS // P * (b + 1))
                if b >= 2:
                    pe.wait_ge(p2_high_kept, b - 1)
                    pe.wait_ge(p2_low_kept, b - 1)
                for j in range(QCOLS // P):
                    last_one = nc.tensor.transpose(turned[:, b % 2, P * j:P * (j + 1)],
                                                   p2[:, QCOLS // P * b + j, :], ident[:])
                last_one.then_inc(p2_turned, 1)

            def multiply(bank, w_high, w_low, x_high, x_low, start, stop):
                nc.tensor.matmul(bank, w_high, x_high, start=start, stop=False)
                nc.tensor.matmul(bank, w_low, x_high, start=False, stop=False)
                return nc.tensor.matmul(bank, w_high, x_low, start=False, stop=stop)

            def make_h1(b):
                cols = slice(QCOLS * b, QCOLS * (b + 1))
                last_p1 = b == BLOCKS - 1
                if last_p1:
                    pe.wait_ge(top_low_made["last_p1"], 1)
                for c in range(C1):
                    if b:
                        pe.wait_ge(h1_high_kept, C1 * (b - 1) + c + 1)
                    o = slice(P * c, P * (c + 1))
                    multiply(parts[:, c, :], wt1_high[:, o], wt1_low[:, o],
                             last_p1_parts[:, 0, :] if last_p1 else p1_high[:, cols],
                             last_p1_parts[:, 1, :] if last_p1 else p1_low[:, cols],
                             start=True, stop=False)
                    if b == 0 and c == 0:
                        pe.wait_ge(dense_copied, 64)
                    nc.tensor.matmul(parts[:, c, :], wt1_dense_parts[:, o], dense_parts[:, cols],
                                     start=False, stop=False)
                pe.wait_ge(p2_high_kept, b + 1)
                pe.wait_ge(p2_low_kept, b + 1)
                for c in range(C1):
                    o = slice(H1 + P * c, H1 + P * (c + 1))
                    multiply(parts[:, c, :], wt1_high[:, o], wt1_low[:, o], p2_high[:, cols], p2_low[:, cols],
                             start=False, stop=True).then_inc(h1_made, 1)

            def make_h2(b):
                if b == 0:
                    pe.wait_ge(top_low_made["wt2"], 2)
                if b:
                    pe.wait_ge(h2_kept, C2 * b)
                for k in range(C1):
                    pe.wait_ge(h1_high_kept, C1 * b + k + 1)
                    pe.wait_ge(h1_low_kept, C1 * b + k + 1)
                    for c in range(C2):
                        bank = parts[:, 4, :] if c == 0 else x1_sum[:]
                        o = slice(H2 * k + P * c, H2 * k + P * (c + 1))
                        low_at = slice(H2 * (k % 2) + P * c, H2 * (k % 2) + P * (c + 1))
                        w_low = wt2_low[k // 2][:, low_at]
                        last_one = multiply(bank, wt2_high[:, o], w_low, h1_high[:, k, :], h1_low[:, k, :],
                                            start=(k == 0), stop=(k == C1 - 1))
                    last_one.then_inc(h1_used, 1)

            def make_y(b):
                pe.wait_ge(p2_high_kept, BLOCKS)
                pe.wait_ge(p2_low_kept, BLOCKS)
                if b >= 2:
                    pe.wait_ge(y_kept, b - 1)
                for k in range(C2):
                    pe.wait_ge(h2_kept, C2 * b + k + 1)
                    last_one = nc.tensor.matmul(turned[0:1, b % 2, :], wt3_sb[:, k:k + 1], h2_sb[:, b % 2, k, :],
                                                start=(k == 0), stop=(k == C2 - 1))
                last_one.then_inc(y_made, 1)

            turn_p2(0)
            turn_p2(1)
            pe.wait_ge(terms_added, TILES * SLABS * D_TERMS)
            pe.wait_ge(parts_scaled, TILES * SLABS * NA)
            pe.wait_ge(top_low_made["wt1"], TOP_PIECES["wt1"])
            pe.wait_ge(top_low_made["p1"], TOP_PIECES["p1"])
            for step in range(BLOCKS + 2):
                if step < BLOCKS:
                    make_h1(step)
                if step < 2:
                    turn_p2(step + 2)
                if 0 <= step - 1 < BLOCKS:
                    make_h2(step - 1)
                if 0 <= step - 2 < BLOCKS:
                    make_y(step - 2)


def kernel(**inputs):
    import numpy as np
    import concourse.bacc as bacc
    from concourse.bass_utils import run_bass_kernel_spmd

    nc = bacc.Bacc("TRN2", target_bir_lowering=False, num_devices=1)
    arrays = {}

    def given(name, a):
        a = np.ascontiguousarray(a)
        arrays[name] = a
        return nc.dram_tensor(name, a.shape, mybir.dt.from_np(a.dtype), kind="ExternalInput").ap()

    W1 = np.asarray(inputs["L0_rec_W1"])
    w1_a = np.zeros((P, CHUNKS, S1), W1.dtype)
    w1_b = np.zeros((P, CHUNKS, S1), W1.dtype)
    w1_rest_a = np.zeros((REST, S1), W1.dtype)
    w1_rest_b = np.zeros((REST, S1), W1.dtype)
    places = [(w1_a[:, c], w1_b[:, c], run) for c in range(CHUNKS) for run in chunk_runs(c)]
    row = 0
    for m, partner, n in REST_RUNS:
        places.append((w1_rest_a, w1_rest_b, (row, m, partner, n)))
        row += n
    for a, b, (row, m, partner, n) in places:
        for i in range(n):
            f, g = m + i, (partner + i) % FIELDS
            a[row + i] = W1[:, f, g]
            if f != g:
                b[row + i] = W1[:, g, f]

    W2 = np.asarray(inputs["L0_rec_W2"])
    args = [
        given("dense_t", np.asarray(inputs["dense_ctx"]).T),
        given("ids", np.asarray(inputs["ids"])),
        [given(f"tbl_{f}", np.asarray(inputs[f"tbl_{f}"])) for f in range(FIELDS)],
        given("w1_a", w1_a),
        given("w1_b", w1_b),
        given("w1_rest_a", w1_rest_a),
        given("w1_rest_b", w1_rest_b),
        given("b1", np.asarray(inputs["L0_rec_b1"]).reshape(S1, 1)),
        given("w2_t", W2.transpose(1, 2, 0).reshape(S1, FIELDS * S2)),
        given("b2", np.asarray(inputs["L0_rec_b2"])),
        given("wt1", np.asarray(inputs["W_top1"])),
        given("bt1", np.asarray(inputs["b_top1"]).reshape(H1 // P, P).T),
        given("wt2", np.asarray(inputs["W_top2"])),
        given("bt2", np.asarray(inputs["b_top2"]).reshape(H2 // P, P).T),
        given("wt3", np.asarray(inputs["W_top3"]).reshape(H2 // P, P).T),
    ]
    spread_from = nc.dram_tensor("spread_from", (2, XFIELDS, QCOLS), mybir.dt.float32, kind="Internal").ap()
    out = nc.dram_tensor("y", (1, BATCH), mybir.dt.float32, kind="ExternalOutput").ap()
    dlrm_tower(nc, *args, spread_from, out)
    r = run_bass_kernel_spmd(nc, [arrays], core_ids=[0])
    return r.results[0]["y"].reshape(BATCH, 1)
```
